# Optimizing a Trainium2 kernel written in Bass

```python
import numpy as np
import jax
import jax.numpy as jnp

def _softmax(x, axis=-1):
    return jax.nn.softmax(x, axis=axis)

def _gelu(x):
    return jax.nn.gelu(x, approximate=True)

def _silu(x):
    return jax.nn.silu(x)

def _sigmoid(x):
    return jax.nn.sigmoid(x)

def _layernorm(x, axis=-1, eps=1e-05):
    m = jnp.mean(x, axis=axis, keepdims=True)
    v = jnp.var(x, axis=axis, keepdims=True)
    return (x - m) / jnp.sqrt(v + eps)

def _scatter_add(tgt, idx, src, axis=0):
    return tgt.at[idx].add(src)

def _segment_sum(src, seg, n):
    return jax.ops.segment_sum(src, seg, n)
kernel_name = 'mk_adaln_d1_jaxref_r8_3bbc98'

def setup_inputs(seed: int=0):
    np.random.seed(seed)
    _w = jnp.asarray

    def _L0_attn_setup():
        import jax, jax.numpy as jnp
        import numpy as np
        EPS = 1e-06
        key = jax.random.key(seed)
        ks = jax.random.split(key, 8)
        b, n, d, h = (2, 256, 128, 16)
        std = 0.02
        x = jax.random.normal(ks[0], (b, n, d), jnp.float32)
        Wq = jax.random.normal(ks[1], (d, d), jnp.float32) * std
        Wk = jax.random.normal(ks[2], (d, d), jnp.float32) * std
        Wv = jax.random.normal(ks[3], (d, d), jnp.float32) * std
        Wo = jax.random.normal(ks[4], (d, d), jnp.float32) * std
        Wbet = jax.random.normal(ks[5], (d, h), jnp.float32) * std
        Wf = jax.random.normal(ks[6], (d, h), jnp.float32) * std
        norm_w = jnp.ones((d,), jnp.float32)
        return {'x': x, 'Wq': Wq, 'Wk': Wk, 'Wv': Wv, 'Wo': Wo, 'Wbet': Wbet, 'Wf': Wf, 'norm_w': norm_w}
    _L0_attn_in = _L0_attn_setup()

    def _L0_ffn_setup():
        import jax, jax.numpy as jnp
        import numpy as np
        B, S, DIM, FFN, E = (4, 256, 128, 512, 8)
        key = jax.random.key(seed)
        k0, k1, k2, k3 = jax.random.split(key, 4)
        scale = 0.02
        return {'hidden_states': jax.random.normal(k0, (B, S, DIM), jnp.float32), 'router_w': jax.random.normal(k1, (DIM, E), jnp.float32) * scale, 'router_b': jnp.zeros((E,), jnp.float32), 'w1': jax.random.normal(k2, (E, DIM, 2 * FFN), jnp.float32) * scale, 'w2': jax.random.normal(k3, (E, FFN, DIM), jnp.float32) * scale}
    _L0_ffn_in = _L0_ffn_setup()
    _L0_c = _w((lambda *s: np.random.randn(*s).astype(np.float32) * 0.05)(16, 128))
    _L0_wmod = _w((lambda *s: np.random.randn(*s).astype(np.float32) * 0.05)(128, 6 * 128) * 128 ** (-0.5))
    _d = {'L0_attn_x': _L0_attn_in['x'], 'L0_attn_Wq': _L0_attn_in['Wq'], 'L0_attn_Wk': _L0_attn_in['Wk'], 'L0_attn_Wv': _L0_attn_in['Wv'], 'L0_attn_Wo': _L0_attn_in['Wo'], 'L0_attn_Wbet': _L0_attn_in['Wbet'], 'L0_attn_Wf': _L0_attn_in['Wf'], 'L0_attn_norm_w': _L0_attn_in['norm_w'], 'L0_ffn_router_w': _L0_ffn_in['router_w'], 'L0_ffn_router_b': _L0_ffn_in['router_b'], 'L0_ffn_w1': _L0_ffn_in['w1'], 'L0_ffn_w2': _L0_ffn_in['w2'], 'L0_c': _L0_c, 'L0_wmod': _L0_wmod}
    _x0 = _d['L0_attn_x']
    _d['L0_attn_x'] = jax.random.normal(jax.random.fold_in(jax.random.key(seed), 1), (16, 256, 128), dtype=_x0.dtype)
    del _x0
    return _d

def reference(L0_attn_x, L0_attn_Wq, L0_attn_Wk, L0_attn_Wv, L0_attn_Wo, L0_attn_Wbet, L0_attn_Wf, L0_attn_norm_w, L0_ffn_router_w, L0_ffn_router_b, L0_ffn_w1, L0_ffn_w2, L0_c, L0_wmod):

    def _L0_attn_ref(x, Wq, Wk, Wv, Wo, Wbet, Wf, norm_w):
        import jax, jax.numpy as jnp
        import numpy as np
        EPS = 1e-06
        b, n, d = x.shape
        h = Wbet.shape[1]
        hd = d // h
        q = jax.nn.silu(x @ Wq).reshape(b, n, h, hd)
        k = jax.nn.silu(x @ Wk).reshape(b, n, h, hd)
        k = k * jax.lax.rsqrt(jnp.sum(k * k, -1, keepdims=True) + 1e-12)
        v = (x @ Wv).reshape(b, n, h, hd)
        beta = 2.0 * jax.nn.sigmoid(x @ Wbet)
        a = jax.nn.sigmoid(x @ Wf)

        def step(S, inp):
            qt, kt, vt, at, bt = inp
            Sd = at[..., None, None] * S
            u = vt - jnp.einsum('bhk,bhkv->bhv', kt, Sd)
            Sn = Sd + bt[..., None, None] * kt[..., None] * u[:, :, None, :]
            o = jnp.einsum('bhk,bhkv->bhv', qt, Sn)
            return (Sn, o)
        tfirst = lambda z: jnp.moveaxis(z, 1, 0)
        S0 = jnp.zeros((b, h, hd, hd), x.dtype)
        _, o = jax.lax.scan(step, S0, (tfirst(q), tfirst(k), tfirst(v), tfirst(a), tfirst(beta)))
        o = jnp.moveaxis(o, 0, 1)
        o = o * jax.lax.rsqrt(jnp.mean(o * o, -1, keepdims=True) + EPS)
        o = o.reshape(b, n, d) * norm_w
        return o @ Wo

    def _L0_ffn_ref(hidden_states, router_w, router_b, w1, w2):
        import jax, jax.numpy as jnp
        import numpy as np
        B, S, DIM, FFN, E = (4, 256, 128, 512, 8)
        b, s, d = hidden_states.shape
        x = hidden_states.reshape(-1, d)
        logits = x @ router_w + router_b
        route = jax.nn.softmax(logits, axis=1)
        max_prob = jnp.max(route, axis=1, keepdims=True)
        max_ind = jnp.argmax(route, axis=1)
        out = jnp.zeros_like(x)
        num_experts = w1.shape[0]
        for e in range(num_experts):
            h = x @ w1[e]
            a, g = jnp.split(h, 2, axis=1)
            y = jax.nn.silu(a) * g @ w2[e]
            out = jnp.where((max_ind == e)[:, None], y, out)
        out = out * max_prob
        return out.reshape(b, s, d)
    x = L0_attn_x
    mod = (_silu(L0_c) @ L0_wmod).reshape(L0_c.shape[0], 6, 1, -1)
    sa, ca, ga, sb, cb, gb = (mod[:, 0], mod[:, 1], mod[:, 2], mod[:, 3], mod[:, 4], mod[:, 5])
    ga = (2 * (ga >= 0) - 1) * jnp.maximum(jnp.abs(ga), 0.25)
    gb = (2 * (gb >= 0) - 1) * jnp.maximum(jnp.abs(gb), 0.25)
    h = _layernorm(x, axis=-1) * (1 + ca) + sa
    x = x + ga * _L0_attn_ref(h, L0_attn_Wq, L0_attn_Wk, L0_attn_Wv, L0_attn_Wo, L0_attn_Wbet, L0_attn_Wf, L0_attn_norm_w)
    h = _layernorm(x, axis=-1) * (1 + cb) + sb
    x = x + gb * _L0_ffn_ref(h, L0_ffn_router_w, L0_ffn_router_b, L0_ffn_w1, L0_ffn_w2)
    return x

_drawn_inputs = setup_inputs


def setup_inputs(seed=0):
    import zlib

    import numpy as np

    out = dict(_drawn_inputs(seed))
    spreads = {'L0_attn_norm_w': (1.0, 0.6), 'L0_ffn_router_b': (0.0, 0.8)}
    factors = {'L0_attn_Wbet': 8.0,
     'L0_attn_Wf': 8.0,
     'L0_ffn_router_w': 8.0,
     'L0_ffn_w1': 8.0,
     'L0_ffn_w2': 8.0}
    for name, (base, spread) in spreads.items():
        noise = np.random.default_rng([zlib.crc32(name.encode()), seed]).standard_normal(out[name].shape)
        drawn = base * np.exp(spread * noise) if base else spread * noise
        out[name] = jnp.asarray(drawn.astype(out[name].dtype))
    for name, factor in factors.items():
        out[name] = (out[name] * factor).astype(out[name].dtype)
    return out
```

```python
from contextlib import ExitStack

import concourse.bass as bass
from concourse import mybir

F32 = mybir.dt.float32
I32 = mybir.dt.int32
U32 = mybir.dt.uint32
ALU = mybir.AluOpType
ACT = mybir.ActivationFunctionType
AX_X = mybir.AxisListType.X

P = 128
LN_EPS = 1e-5
K_EPS = 1e-12
O_EPS = 1e-6


def adaln_block(nc, x, Wq, Wk, Wv, Wo, Wbet, Wf, norm_w, router_w, router_b, w1, w2, c, wmod, out):
    B, N, D = x.shape
    H = Wbet.shape[1]
    HD = D // H
    E, _, F2 = w1.shape
    FF = F2 // 2
    FC = FF // P
    NHALF = 2
    HB = B // NHALF
    assert HB * H == P and N == 2 * P and D == P
    NT = HB * N // P
    PC = 4
    CT = NT // PC
    CW = CT * P
    C = 4
    NCH = N // C
    GC = 4
    NG = NCH // GC
    SR = 16
    UR = 4
    NS = HD + C
    NF = NT + E - 1
    NFE = NF * P

    sorted_h = [nc.dram_tensor(f"sorted_h{h}", (NFE, D), F32, kind="Internal").ap() for h in range(NHALF)]
    sorted_y = [nc.dram_tensor(f"sorted_y{h}", (NFE, D), F32, kind="Internal").ap() for h in range(NHALF)]
    x_t = x.rearrange("b (s p) d -> p (b s) d", p=P)
    out_t = out.rearrange("b (s p) d -> p (b s) d", p=P)

    with ExitStack() as ctx:
        def sb(name, shape, dt=F32):
            return ctx.enter_context(nc.sbuf_tensor(name, shape, dt))

        sems = {}

        def sem(name, h=None):
            key = name if h is None else f"{name}{h}"
            if key not in sems:
                sems[key] = ctx.enter_context(nc.semaphore(key))
            return sems[key]

        X = sb("X", [P, B * N // P, D])
        XN = sb("XN", [P, NT, D])
        big = sb("big", [P, 12288])
        RAW = big[:, 0:6144].rearrange("p (d x t) -> p d x t", d=HD, x=3)
        TMP = big[:, 6144:9216]
        QKV = big[:, 9216:12288].rearrange("p (r b x t) -> p r b x t", r=2, b=2, x=3)
        W1 = big[:, 0:E * F2].rearrange("p (e f) -> p e f", e=E)
        W2 = big[:, E * F2:12288].rearrange("p (e c d) -> p e c d", e=E, c=FC)
        ph = sb("ph", [P, 2048])
        HT = ph[:, 0:1024].rearrange("p (r t) -> p r t", r=2)
        BFT = ph[:, 1024:2048].rearrange("p (r b t) -> p r b t", r=2, b=2)
        WOG = ph[:, :].rearrange("p (b d) -> p b d", b=B)
        WP = sb("WP", [P, 3, D])
        WBF = sb("WBF", [P, H, 2])
        WBFR = sb("WBFR", [P, 2, H])
        WO = sb("WO", [P, D])
        NW = sb("NW", [P, 1])
        RW = sb("RW", [P, E])
        RB = sb("RB", [P, E])
        CT_ = sb("CT_", [P, B])
        MOD = sb("MOD", [P, 4, B])
        GATE = sb("GATE", [B, 2, D])
        ID = sb("ID", [P, P])
        LOWER = sb("LOWER", [P, P])
        ONES = sb("ONES", [P, P])
        prod_o = sb("prod_o", [P, 2, NS, GC * C * HD])
        K_ = [sb(f"K{h}", [P, N, HD]) for h in range(NHALF)]
        Q_ = [sb(f"Q{h}", [P, N, HD]) for h in range(NHALF)]
        X_ = [sb(f"X{h}", [P, N, 2 * HD]) for h in range(NHALF)]
        PD = [sb(f"PD{h}", [P, C, N]) for h in range(NHALF)]
        GAM = [sb(f"GAM{h}", [P, NCH]) for h in range(NHALF)]
        S_ = [sb(f"S{h}", [P, SR, HD, HD]) for h in range(NHALF)]
        p1 = [sb(f"p1{h}", [P, UR, C, HD, HD + 1]) for h in range(NHALF)]
        p2 = [sb(f"p2{h}", [P, HD, HD, C + 1]) for h in range(NHALF)]
        sm = sb("sm", [P, 8, N])
        st = sb("st", [P, NT, 6])
        mv = sb("mv", [P, NT, 2])
        ve = sb("ve", [P, NT])
        sd = sb("sd", [P, NT])
        yy = sb("yy", [P, NT])
        y2 = sb("y2", [P, NT])
        lg = sb("lg", [P, NT, E])
        lm = sb("lm", [P, NT])
        lmx = sb("lmx", [P, NT])
        oh = sb("oh", [P, NT, E])
        t8 = sb("t8", [P, NT, E])
        tot = sb("tot", [P, E, NT])
        exc = sb("exc", [P, E, NT])
        msk = sb("msk", [P, E, NT])
        rev = sb("rev", [P, E])
        i128 = sb("i128", [P, NT])
        ij = sb("ij", [P, NF])
        one8 = sb("one8", [P, E])
        nt8 = sb("nt8", [P, E])
        cu8 = sb("cu8", [P, E])
        ba8 = sb("ba8", [P, E])
        cmp = sb("cmp", [P, NF, E])
        cmn = sb("cmn", [P, E, NT])
        texf = sb("texf", [P, NF])
        posf = sb("posf", [P, NT])
        maxp = [sb(f"maxp{h}", [P, NT]) for h in range(NHALF)]
        tex = [sb(f"tex{h}", [P, NF], I32) for h in range(NHALF)]
        pos = [sb(f"pos{h}", [P, NT], U32) for h in range(NHALF)]

        bank = [ctx.enter_context(nc.psum_tensor(f"bank{i}", [P, 512], F32)) for i in range(8)]

        block = ctx.enter_context(nc.Block())

        k1 = K_[1][:, :, :].rearrange("p t d -> p (t d)")
        WM = k1[:, 0:6 * D].rearrange("p (j f) -> p j f", j=6)
        CROW = k1[0:B, 6 * D:7 * D]
        CE = k1[0:B, 7 * D:8 * D]
        GTMP = k1[0:B, 8 * D:10 * D].rearrange("p (j d) -> p j d", j=2)
        po1 = prod_o[:, 1, :, :].rearrange("p a b -> p (a b)")
        L = po1[:, 0:NCH * C * C].rearrange("p (n a) -> p n a", n=NCH)
        BA = po1[:, NCH * C * C:NCH * C * C + 2 * N].rearrange("p (x t) -> p x t", x=2)
        OT = [X_[h][:, 0:P, :].rearrange("p t d -> p (t d)").rearrange("p (b t) -> p b t", b=HB) for h in range(NHALF)]
        H2 = [Q_[h][:, :, :].rearrange("p t d -> p (t d)").rearrange("p (n d) -> p n d", n=NT) for h in range(NHALF)]
        YG = [K_[h][:, :, :].rearrange("p t d -> p (t d)").rearrange("p (n d) -> p n d", n=NT) for h in range(NHALF)]
        OV = [Q_[h][:, :, :].rearrange("p t d -> p (t d)").rearrange("p (v t) -> p v t", v=HD) for h in range(NHALF)]
        SQO = XN[:, :, :].rearrange("p n d -> p (n d)").rearrange("p (t v) -> p t v", v=HD)
        fx = X_[0][:, P:2 * P, :].rearrange("p t d -> p (t d)")
        XS = fx[:, 0:512].rearrange("p (r d) -> p r d", r=4)
        XST = fx[:, 512:768].rearrange("p (r d) -> p r d", r=2)
        YS = fx[:, 768:1280].rearrange("p (r d) -> p r d", r=4)
        fz = X_[1][:, P:2 * P, :].rearrange("p t d -> p (t d)")
        GU = fz[:, 0:1024].rearrange("p (r f) -> p r f", r=2)
        GUT = fz[:, 1024:2048].rearrange("p (r f) -> p r f", r=2)
        ZERO = prod_o[:, 0, :, :].rearrange("p a b -> p (a b)")[:, 0:D]
        H2T = prod_o[:, 0, :, :].rearrange("p a b -> p (a b)")[:, 0:1024].rearrange("p (r t) -> p r t", r=2)
        NW_LOADS = 9

        def stores(g):
            return len([i for i in range(g // NF * NF, g + 1) if i % 4 == g % 4])

        def store_y(sp, g):
            h, j = divmod(g, NF)
            sp.wait_ge(sem("ys_ready"), g + 1)
            sp.dma_start(sorted_y[h][j * P:(j + 1) * P, :], YS[:, g % 4, :]).then_inc(sem(f"ys_out{g % 4}_", h), 16)

        @block.sync
        def _(sp):
            sp.dma_start(CROW[:, :], c).then_inc(sem("c_in"), 16)
            sp.dma_start(WM[:, :, :], wmod.rearrange("d (j f) -> d j f", j=6)).then_inc(sem("wm_in"), 16)
            for i in range(8):
                sp.dma_start(X[:, 4 * i:4 * i + 4, :], x_t[:, 4 * i:4 * i + 4, :]).then_inc(sem(f"x_in{i}"), 16)
            for i, w in enumerate((Wq, Wk, Wv)):
                sp.dma_start(WP[:, i, :], w).then_inc(sem("w_in"), 16)
            sp.dma_start(WBFR[:, 0, :], Wbet).then_inc(sem("w_in"), 16)
            sp.dma_start(WBFR[:, 1, :], Wf).then_inc(sem("w_in"), 16)
            sp.dma_start(WO[:, :], Wo).then_inc(sem("w_in"), 16)
            sp.dma_start(NW[:, :], norm_w.rearrange("(p a) -> p a", a=1)).then_inc(sem("w_in"), 16)
            sp.dma_start(RW[:, :], router_w).then_inc(sem("w_in"), 16)
            sp.dma_start(RB[:, :], router_b.rearrange("(a e) -> a e", a=1).broadcast_to([P, E])).then_inc(sem("w_in"), 16)
            sp.wait_ge(sem("const_set"), 1)
            for h in range(NHALF):
                sp.dma_start(sorted_h[h].rearrange("(n p) d -> p n d", p=P), ZERO.unsqueeze(1).broadcast_to([P, NF, D])).then_inc(sem("zeroed", h), 16)

            for h in range(NHALF):
                for pc in range(PC):
                    for b2 in range(2):
                        b = 2 * pc + b2
                        if b2 == 0:
                            sp.wait_ge(sem("qk_evac", h), 3 * (pc + 1))
                            sp.wait_ge(sem("v_evac", h), pc + 1)
                        if h == 1 and pc == 0 and b2 == 0:
                            sp.wait_ge(sem("q_raw", 0), 1)
                            sp.wait_ge(sem("raw_used"), 2)
                        r = pc % 2
                        sp.dma_start(RAW[b * H:(b + 1) * H, :, :, :], QKV[:, r, b2, :, :]).then_inc(sem(f"raw_in{r}_", h), 16)
                        sp.dma_start(BA[b * H:(b + 1) * H, :, :], BFT[0:2 * H, r, b2, :]).then_inc(sem(f"raw_in{r}_", h), 16)
            sp.wait_ge(sem("prep_done", 1), 1)
            sp.dma_start(W1, w1.rearrange("e d f -> d e f")).then_inc(sem("w1_in"), 16)
            sp.dma_start(W2, w2.rearrange("e (c p) d -> p e c d", p=P)).then_inc(sem("w2_in"), 16)
            for h in range(NHALF):
                sp.wait_ge(sem("ov_ready", h), 1)
                sp.wait_ge(sem("prod_ready", h), NG)
                for b in range(HB):
                    sp.dma_start(OT[h][:, b, :], OV[h][b * H:(b + 1) * H, :, :]).then_inc(sem("ot_in", h), 16)
            for h in range(NHALF):
                sp.wait_ge(sem("scattered", h), 16 * NT)
                for j in range(NF):
                    g = h * NF + j
                    if g >= 4:
                        sp.wait_ge(sem("xs_used"), g - 3)
                    sp.dma_start(XS[:, g % 4, :], sorted_h[h][j * P:(j + 1) * P, :]).then_inc(sem(f"xs_in{g % 4}"), 16)
                    if g >= 3:
                        store_y(sp, g - 3)
            for g in range(NHALF * NF - 3, NHALF * NF):
                store_y(sp, g)
            for h in range(NHALF):
                for q in range(4):
                    sp.wait_ge(sem("out_ready", h), q + 1)
                    t0 = h * NT + 4 * q
                    sp.dma_start(out_t[:, t0:t0 + 4, :], X[:, t0:t0 + 4, :]).then_inc(sem("stored"), 16)
            sp.wait_ge(sem("stored"), 16 * 8)

        @block.tensor
        def _(pe):
            pe.wait_ge(sem("const_set"), 1)
            pe.wait_ge(sem("ce_ready"), 1)
            pe.transpose(bank[0][:, 0:B], CE[:, :], ID[0:B, 0:B]).then_inc(sem("ct_ps"), 1)
            pe.wait_ge(sem("ct_ready"), 1)
            pe.wait_ge(sem("wm_in"), 16)
            for i, j in enumerate((0, 1, 3, 4)):
                m = pe.matmul(bank[1][:, i * B:(i + 1) * B], WM[:, j, :], CT_[:, :], start=True, stop=True)
            m.then_inc(sem("mod_ps"), 1)
            for i, j in enumerate((2, 5)):
                m = pe.matmul(bank[2][0:B, i * D:(i + 1) * D], CT_[:, :], WM[:, j, :], start=True, stop=True)
            m.then_inc(sem("gate_ps"), 1)

            def project(h, pc):
                k = h * PC + pc
                pe.wait_ge(sem("xn_ready", h), CT * (pc + 1))
                if k >= 1:
                    pe.wait_ge(sem("ht_evac"), 2 * k)
                else:
                    pe.wait_ge(sem("ct_ready"), 1)
                for i in range(CT):
                    m = pe.transpose(bank[0][:, i * P:(i + 1) * P], XN[:, pc * CT + i, :], ID[:, :])
                m.then_inc(sem("xnt_ps"), 1)
                pe.wait_ge(sem("ht_evac"), 2 * (k + 1))
                if k == 0:
                    pe.wait_ge(sem("w_in"), 16 * NW_LOADS)
                    pe.wait_ge(sem("wbf_ready"), 1)
                    pe.wait_ge(sem("mod_ready"), 3)
                    pe.wait_ge(sem("gate_ready"), 1)
                rhs = HT[:, k % 2, :]
                for i in range(3):
                    if k >= 1:
                        if i < 2:
                            pe.wait_ge(sem("qk_evac", (k - 1) // PC), 3 * ((k - 1) % PC) + i + 1)
                        else:
                            pe.wait_ge(sem("v_evac", (k - 1) // PC), (k - 1) % PC + 1)
                    pe.matmul(bank[1 + i][:, :], WP[:, i, :], rhs, start=True, stop=True).then_inc(sem("proj_ps"), 1)
                if k >= 1:
                    pe.wait_ge(sem("qk_evac", (k - 1) // PC), 3 * ((k - 1) % PC) + 3)
                pe.matmul(bank[4][0:2 * H, :], WBF[:, :, :].rearrange("p h x -> p (h x)"), rhs, start=True, stop=True)\
                    .then_inc(sem("proj_ps"), 1)

            for h in range(NHALF):
                for pc in range(PC):
                    project(h, pc)

            for b in range(B):
                if b >= 2:
                    pe.wait_ge(sem("wog_ready"), b - 1)
                else:
                    pe.wait_ge(sem("qk_evac", 1), 3 * PC)
                pe.matmul(bank[5 + b % 2][:, 0:D], ID[0:B, b:b + 1].broadcast_to([B, P]), GATE[:, 0, :], start=True, stop=True).then_inc(sem("ga_ps"), 1)

            pe.wait_ge(sem("wog_ready"), B)
            for g in range(NG):
                for h in range(NHALF):
                    k = g * NHALF + h
                    pe.wait_ge(sem("prod_ready", h), g + 1)
                    if k >= 2:
                        pe.wait_ge(sem("o_evac"), k - 1)
                    ps = bank[5 + k % 2][:, 0:GC * C * HD]
                    for s in range(HD):
                        pe.matmul(ps, ID[:, :], prod_o[:, k % 2, s, :], start=(s == 0), stop=False, skip_group_check=True)
                    for d in range(C):
                        o4 = ps.rearrange("p (n i v) -> p n i v", n=GC, i=C)[:, :, d:C, :]
                        r4 = prod_o[:, k % 2, HD + d, :].rearrange("p (n i v) -> p n i v", n=GC, i=C)[:, :, d:C, :]
                        m = pe.matmul(o4, ID[:, :], r4, start=False, stop=(d == C - 1), skip_group_check=True)
                    m.then_inc(sem("o_ps"), 1)

            for h in range(NHALF):
                pe.wait_ge(sem("ot_in", h), 16 * HB)
                for q in range(4):
                    k = 4 * h + q
                    if k >= 2:
                        pe.wait_ge(sem("x1_ready"), k - 1)
                    else:
                        pe.wait_ge(sem("o_evac"), NG * NHALF)
                    for i in range(4):
                        t = 4 * q + i
                        m = pe.matmul(bank[5 + k % 2][:, i * P:(i + 1) * P], OT[h][:, t // 2, (t % 2) * P:(t % 2 + 1) * P],
                                      WOG[:, h * HB + t // 2, :], start=True, stop=True)
                    m.then_inc(sem("att_ps"), 1)

            for h in range(NHALF):
                for pc in range(PC):
                    k = h * PC + pc
                    pe.wait_ge(sem("xn2_ready", h), CT * (pc + 1))
                    if k >= 1:
                        pe.wait_ge(sem("h2t_evac"), 2 * k)
                    for i in range(CT):
                        m = pe.transpose(bank[0][:, i * P:(i + 1) * P], XN[:, pc * CT + i, :], ID[:, :])
                    m.then_inc(sem("xn2t_ps"), 1)
                    pe.wait_ge(sem("h2t_evac"), 2 * (k + 1))
                    if h == 1 and pc == 0:
                        pe.wait_ge(sem("lg_ready", 0), 1)
                    for i in range(CT):
                        t = pc * CT + i
                        m = pe.matmul(bank[1][:, t * E:(t + 1) * E], H2T[:, k % 2, i * P:(i + 1) * P], RW[:, :], start=True, stop=True)
                    m.then_inc(sem("lg_ps", h), 1)
                    if k >= 1:
                        pe.wait_ge(sem("h2_evac"), k)
                    else:
                        pe.wait_ge(sem("x1_ready"), 8)
                    for i in range(CT):
                        m = pe.transpose(bank[2][:, i * P:(i + 1) * P], H2T[:, k % 2, i * P:(i + 1) * P], ID[:, :])
                    m.then_inc(sem("h2_ps"), 1)
                pe.wait_ge(sem("oh_ready", h), 1)
                ohf = oh[:, :, :].rearrange("p t e -> p (t e)")
                pe.matmul(bank[3][:, 0:NT * E], LOWER[:, :], ohf, start=True, stop=True)
                pe.matmul(bank[4][:, 0:NT * E], ONES[:, :], ohf, start=True, stop=True).then_inc(sem("rank_ps", h), 1)

            pe.wait_ge(sem("w1_in"), 16)
            pe.wait_ge(sem("w2_in"), 16)
            pe.wait_ge(sem("h2_evac"), NHALF * PC)
            G = NHALF * NF
            expert = {}

            def turn_x(g):
                pe.wait_ge(sem(f"xs_in{g % 4}"), 16 * (g // 4 + 1))
                if g >= 1:
                    pe.wait_ge(sem("xst_ready"), g)
                pe.transpose(bank[0][:, 0:P], XS[:, g % 4, :], ID[:, :]).then_inc(sem("xs_used"), 1)

            def hidden(g):
                h, j = divmod(g, NF)
                if j == 0:
                    pe.wait_ge(sem("tex_ready", h), 1)
                    pe.wait_ge(sem("pos_ready", h), 1)
                expert[g] = pe.value_load(tex[h][0:1, j:j + 1], min_val=0, max_val=E - 1)
                pe.wait_ge(sem("xst_ready"), g + 1)
                for k in range(2):
                    if g >= 2:
                        pe.wait_ge(sem("silu_a") if k == 0 else sem("gu_ready"), g - 1)
                    pe.matmul(bank[(1, 6)[g % 2] + k][:, :], XST[:, g % 2, :],
                              W1[:, bass.ds(expert[g], 1), k * FF:(k + 1) * FF],
                              start=True, stop=True).then_inc(sem("h_ps"), 1)

            def turn_g(g):
                pe.wait_ge(sem("gu_ready"), g + 1)
                if g >= 1:
                    pe.wait_ge(sem("gut_ready"), g)
                for k in range(FC):
                    m = pe.transpose(bank[3][:, k * P:(k + 1) * P], GU[:, g % 2, k * P:(k + 1) * P], ID[:, :])
                m.then_inc(sem("gut_ps"), 1)

            def second(g):
                pe.wait_ge(sem("gut_ready"), g + 1)
                if g >= 1:
                    pe.wait_ge(sem("ys_ready"), g)
                for k in range(FC):
                    m = pe.matmul(bank[4][:, 0:D], GUT[:, g % 2, k * P:(k + 1) * P], W2[:, bass.ds(expert[g], 1), k, :],
                                  start=(k == 0), stop=(k == FC - 1))
                m.then_inc(sem("y_ps"), 1)

            turn_x(0)
            for g in range(G + 2):
                if g < G:
                    hidden(g)
                if g + 1 < G:
                    turn_x(g + 1)
                if 0 <= g - 1 < G:
                    turn_g(g - 1)
                if g >= 2:
                    second(g - 2)
            for b in range(B):
                if b >= 2:
                    pe.wait_ge(sem("gb_used"), b - 1)
                pe.matmul(bank[5 + b % 2][:, 0:D], ID[0:B, b:b + 1].broadcast_to([B, P]), GATE[:, 1, :], start=True, stop=True).then_inc(sem("gb_ps"), 1)


        @block.gpsimd
        def _(pool):
            done = [0]

            def link(ins):
                done[0] += 1
                ins.then_inc(sem("pool_link"), 1)
                pool.wait_ge(sem("pool_link"), done[0])

            pool.memset(ID[:, :], 0.0)
            pool.memset(LOWER[:, :], 1.0)
            pool.memset(ONES[:, :], 1.0)
            pool.memset(ZERO, 0.0)
            pool.memset(one8[:, :], 1.0)
            link(pool.memset(msk[:, :, :], 1.0))
            pool.affine_select(out=ID[:, :], in_=ID[:, :], compare_op=ALU.not_equal, fill=1.0, base=0,
                               pattern=[[-1, P]], channel_multiplier=1)
            pool.affine_select(out=LOWER[:, :], in_=LOWER[:, :], compare_op=ALU.is_gt, fill=0.0, base=0,
                               pattern=[[1, P]], channel_multiplier=-1)
            pool.memset(msk[:, :, 0:1], 0.0)
            pool.iota(rev[:, :], [[-1, E]], base=E, channel_multiplier=0, allow_small_or_imprecise_dtypes=True)
            pool.iota(i128[:, :], [[P, NT]], base=0, channel_multiplier=0, allow_small_or_imprecise_dtypes=True)
            pool.iota(ij[:, :], [[1, NF]], base=0, channel_multiplier=0, allow_small_or_imprecise_dtypes=True)\
                .then_inc(sem("const_set"), 1)

            for g in range(NG):
                for h in range(NHALF):
                    k = g * NHALF + h
                    if k >= 2:
                        pool.wait_ge(sem("o_ps"), k - 1)
                    elif k == 0:
                        for hh in range(NHALF):
                            pool.wait_ge(sem("zeroed", hh), 16)
                            pool.wait_ge(sem("prep_done", hh), 1)
                    slot = prod_o[:, k % 2, :, :].rearrange("p s (n i v) -> p s n i v", n=GC, i=C)
                    for m in range(GC):
                        n = g * GC + m
                        pool.wait_ge(sem("s_ready", h), n + 1)
                        q = Q_[h][:, n * C:(n + 1) * C, :].rearrange("p i k -> p k i").unsqueeze(3).broadcast_to([P, HD, C, HD])
                        s_ = S_[h][:, n % SR, :, :].rearrange("p v k -> p k v").unsqueeze(2).broadcast_to([P, HD, C, HD])
                        pool.tensor_tensor(slot[:, 0:HD, m, :, :], q, s_, ALU.mult)
                    pool.wait_ge(sem("u_ready", h), (g + 1) * GC)
                    u = X_[h][:, :, 0:HD].rearrange("p (n i) v -> p n i v", i=C)[:, g * GC:(g + 1) * GC, :, :]
                    for d in range(C):
                        w = PD[h][:, d, :].rearrange("p (n i) -> p n i", i=C)[:, g * GC:(g + 1) * GC, d:C]
                        last = pool.tensor_tensor(slot[:, HD + d, :, d:C, :], w.unsqueeze(3).broadcast_to([P, GC, C - d, HD]),
                                                  u[:, :, 0:C - d, :], ALU.mult)
                    last.then_inc(sem("prod_ready", h), 1)

            for h in range(NHALF):
                pool.wait_ge(sem("pos_ready", h), 1)
                pool.wait_ge(sem("h2_evac"), PC * (h + 1))
                for t in range(NT):
                    pool.indirect_dma_start(sorted_h[h], bass.IndirectOffsetOnAxis(ap=pos[h][:, t:t + 1], axis=0),
                                            H2[h][:, t, :], None).then_inc(sem("scattered", h), 16)
            for h in range(NHALF):
                for g in range((h + 1) * NF - 4, (h + 1) * NF):
                    pool.wait_ge(sem(f"ys_out{g % 4}_", h), 16 * stores(g))
                for t in range(NT):
                    pool.indirect_dma_start(YG[h][:, t, :], None, sorted_y[h],
                                            bass.IndirectOffsetOnAxis(ap=pos[h][:, t:t + 1], axis=0))\
                        .then_inc(sem("gathered", h), 16)

        @block.scalar
        def _(act):
            act.wait_ge(sem("c_in"), 16)
            act.activation(CE[:, :], CROW[:, :], ACT.Silu).then_inc(sem("ce_ready"), 1)
            act.wait_ge(sem("ct_ps"), 1)
            act.activation(CT_[:, :], bank[0][:, 0:B], ACT.Copy).then_inc(sem("ct_ready"), 1)
            act.wait_ge(sem("mod_ps"), 1)
            m4 = bank[1][:, 0:4 * B].rearrange("p (j b) -> p j b", j=4)
            act.activation(MOD[:, :, :], m4, ACT.Copy).then_inc(sem("mod_ready"), 1)
            act.wait_ge(sem("mod_ready"), 1)
            for j in (1, 3):
                act.activation(MOD[:, j, :], MOD[:, j, :], ACT.Identity, bias=1.0).then_inc(sem("mod_ready"), 1)

            roots = [0]

            def root(dst, src):
                roots[0] += 1
                act.wait_ge(sem("root_in"), roots[0])
                act.activation(dst, src, ACT.Sqrt).then_inc(sem("root_out"), 1)

            def modulate(dst, k, h, pc, j, done):
                for b2 in range(2):
                    b = h * HB + 2 * pc + b2
                    act.activation(dst[:, k % 2, b2 * N:(b2 + 1) * N], bank[0][:, b2 * N:(b2 + 1) * N], ACT.Identity,
                                   scale=MOD[:, j + 1, b:b + 1], bias=MOD[:, j, b:b + 1]).then_inc(done, 1)

            def evacuate(h, pc):
                k = h * PC + pc
                if k == 0:
                    act.wait_ge(sem("mod_ready"), 3)
                act.wait_ge(sem("xnt_ps"), k + 1)
                if k >= 2:
                    act.wait_ge(sem("proj_ps"), 4 * (k - 1))
                modulate(HT, k, h, pc, 0, sem("ht_evac"))
                if k >= 2:
                    act.wait_ge(sem(f"raw_in{k % 2}_", (k - 2) // PC), 64 * ((k - 2) % PC // 2 + 1))
                for i in range(2):
                    act.wait_ge(sem("proj_ps"), 4 * k + i + 1)
                    act.activation(QKV[:, k % 2, :, i, :], bank[1 + i][:, :].rearrange("p (b t) -> p b t", b=2), ACT.Silu)\
                        .then_inc(sem("qk_evac", h), 1)
                act.wait_ge(sem("proj_ps"), 4 * k + 4)
                act.activation(BFT[0:2 * H, k % 2, :, :], bank[4][0:2 * H, :].rearrange("p (b t) -> p b t", b=2), ACT.Copy)\
                    .then_inc(sem("qk_evac", h), 1)

            def prepare(h):
                for r in range(2):
                    act.wait_ge(sem(f"raw_in{r}_", h), 64 * PC // 2)
                if h == 1:
                    act.wait_ge(sem("prep_done", 0), 1)
                act.activation(TMP[:, 0:N * HD].rearrange("p (t d) -> p t d", d=HD),
                               RAW[:, :, 1, :].rearrange("p d t -> p t d"), ACT.Square).then_inc(sem("ksq"), 1)
                act.activation(Q_[h][:, :, :], RAW[:, :, 0, :].rearrange("p d t -> p t d"), ACT.Copy).then_inc(sem("q_raw", h), 1)
                act.activation(sm[:, 0:2, :], BA[:, :, :], ACT.Sigmoid).then_inc(sem("ba_ready"), 1)
                root(sm[:, 3, :], sm[:, 2, :])

            root(sd[:, :], ve[:, :])
            for pc in range(PC):
                evacuate(0, pc)
            root(sd[:, :], ve[:, :])
            for pc in range(2):
                evacuate(1, pc)
            prepare(0)
            for pc in range(2, PC):
                evacuate(1, pc)
            prepare(1)

            def ubar(h, n):
                if n >= UR:
                    act.wait_ge(sem("u_ready", h), n - UR + 2)
                act.activation(p1[h][:, n % UR:n % UR + 2, :, :, HD],
                               X_[h][:, n * C:(n + 2) * C, 0:HD].rearrange("p (n i) v -> p n i v", n=2), ACT.Copy)\
                    .then_inc(sem("ubar_in", h), 1)

            def decay(h, n):
                act.wait_ge(sem("s_ready", h), n + 1)
                act.activation(p2[h][:, :, :, C], S_[h][:, n % SR, :, :], ACT.Copy, scale=GAM[h][:, n:n + 1])\
                    .then_inc(sem("decayed", h), 1)

            def out_group(g, h):
                k = g * NHALF + h
                act.wait_ge(sem("o_ps"), k + 1)
                act.wait_ge(sem("s_ready", h), min((g + 1) * GC + 1, NCH))
                act.activation(K_[h][:, g * GC * C:(g + 1) * GC * C, :],
                               bank[5 + k % 2][:, 0:GC * C * HD].rearrange("p (t v) -> p t v", v=HD), ACT.Copy)\
                    .then_inc(sem("o_evac"), 1)

            for h in range(NHALF):
                act.wait_ge(sem("prep_done", h), 1)
                ubar(h, 0)
                ubar(h, 2)
            LAGG = 2
            for n in range(NCH):
                if n % 2 == 0 and n >= 2 and n + 2 < NCH:
                    for h in range(NHALF):
                        ubar(h, n + 2)
                for h in range(NHALF):
                    if n < NCH - 1:
                        decay(h, n)
                if n % GC == GC - 1 and n // GC >= LAGG:
                    for h in range(NHALF):
                        out_group(n // GC - LAGG, h)
            for g in range(NG - LAGG, NG):
                for h in range(NHALF):
                    out_group(g, h)

            for h in range(NHALF):
                act.wait_ge(sem("o_evac"), NG * NHALF)
                if h == 1:
                    act.wait_ge(sem("sqo_used"), 1)
                act.activation(SQO[:, :, :], K_[h][:, :, :], ACT.Square).then_inc(sem("sqo"), 1)
                root(sm[:, 3, :], sm[:, 2, :])

            for h in range(NHALF):
                root(sd[:, :], ve[:, :])
                for pc in range(PC):
                    k = h * PC + pc
                    act.wait_ge(sem("xn2t_ps"), k + 1)
                    if k >= 2:
                        act.wait_ge(sem("h2_ps"), k - 1)
                    elif k == 0:
                        act.wait_ge(sem("o_ps"), NG * NHALF)
                    modulate(H2T, k, h, pc, 2, sem("h2t_evac"))
                    act.wait_ge(sem("h2_ps"), k + 1)
                    if pc == 0:
                        act.wait_ge(sem("ot_in", h), 16 * HB)
                    act.activation(H2[h][:, pc * CT:(pc + 1) * CT, :], bank[2][:, :].rearrange("p (n d) -> p n d", n=CT), ACT.Copy)\
                        .then_inc(sem("h2_evac"), 1)
                act.wait_ge(sem("lsub"), h + 1)
                act.activation(t8[:, :, :], t8[:, :, :], ACT.Exp).then_inc(sem("lexp"), 1)

            G = NHALF * NF

            def silu(g):
                act.wait_ge(sem("h_ps"), 2 * g + 1)
                if g >= 2:
                    act.wait_ge(sem("gut_ps"), g - 1)
                act.activation(GU[:, g % 2, :], bank[(1, 6)[g % 2]][:, :], ACT.Silu).then_inc(sem("silu_a"), 1)

            def gut(g):
                act.wait_ge(sem("gut_ps"), g + 1)
                if g >= 2:
                    act.wait_ge(sem("y_ps"), g - 1)
                act.activation(GUT[:, g % 2, :], bank[3][:, :], ACT.Copy).then_inc(sem("gut_ready"), 1)

            for g in range(G + 1):
                if g < G:
                    silu(g)
                if g >= 1:
                    gut(g - 1)

        @block.vector
        def _(dve):
            done = [0]

            def link(ins):
                done[0] += 1
                ins.then_inc(sem("dve_link"), 1)
                dve.wait_ge(sem("dve_link"), done[0])

            roots = [0]

            def rsqrt(var, sroot, y, t):
                link(dve.tensor_copy(y, var))
                roots[0] += 1
                dve.tensor_copy(t, var).then_inc(sem("root_in"), 1)
                dve.wait_ge(sem("root_in"), roots[0])
                dve.wait_ge(sem("root_out"), roots[0])
                link(dve.reciprocal(y, sroot))
                link(dve.tensor_tensor(t, y, y, ALU.mult))
                link(dve.tensor_tensor(t, t, var, ALU.mult))
                link(dve.tensor_scalar(t, t, -0.5, 1.5, ALU.mult, ALU.add))
                link(dve.tensor_tensor(y, y, t, ALU.mult))

            def normalise(h, free, ready):
                for t in range(NT):
                    T = h * NT + t
                    if ready == "xn_ready" and T % 4 == 0:
                        dve.wait_ge(sem(f"x_in{T // 4}"), 16)
                    last = dve.bn_stats(st[:, t, :], X[:, T, :])
                link(last)
                for t in range(NT):
                    last = dve.bn_aggr(mv[:, t, :], st[:, t, :])
                link(last)
                link(dve.tensor_scalar(ve[:, :], mv[:, :, 1], LN_EPS, None, ALU.add))
                rsqrt(ve[:, :], sd[:, :], yy[:, :], y2[:, :])
                free()
                for t in range(NT):
                    dve.tensor_scalar(XN[:, t, :], X[:, h * NT + t, :], mv[:, t, 0:1], yy[:, t:t + 1], ALU.subtract, ALU.mult)\
                        .then_inc(sem(ready, h), 1)
                dve.wait_ge(sem(ready, h), NT)

            dve.wait_ge(sem("w_in"), 16 * NW_LOADS)
            dve.tensor_copy(WBF[:, :, :], WBFR[:, :, :].rearrange("p x h -> p h x")).then_inc(sem("wbf_ready"), 1)
            normalise(0, lambda: None, "xn_ready")
            dve.wait_ge(sem("gate_ps"), 1)
            g2 = bank[2][0:B, 0:2 * D].rearrange("p (j d) -> p j d", j=2)
            link(dve.tensor_copy(GATE[:, :, :], g2))
            link(dve.tensor_scalar(GTMP[:, :, :], GATE[:, :, :], -1.0, 0.25, ALU.mult, ALU.max))
            link(dve.tensor_tensor(GTMP[:, :, :], GTMP[:, :, :], GATE[:, :, :], ALU.max))
            link(dve.tensor_scalar(GATE[:, :, :], GATE[:, :, :], 0.0, 2.0, ALU.is_ge, ALU.mult))
            link(dve.tensor_scalar(GATE[:, :, :], GATE[:, :, :], -1.0, None, ALU.add))
            dve.tensor_tensor(GATE[:, :, :], GATE[:, :, :], GTMP[:, :, :], ALU.mult).then_inc(sem("gate_ready"), 1)

            def values(h, pc):
                k = h * PC + pc
                dve.wait_ge(sem("proj_ps"), 4 * k + 3)
                if k >= 2:
                    dve.wait_ge(sem(f"raw_in{k % 2}_", (k - 2) // PC), 64 * ((k - 2) % PC // 2 + 1))
                dve.tensor_copy(QKV[:, k % 2, :, 2, :], bank[3][:, :].rearrange("p (b t) -> p b t", b=2))\
                    .then_inc(sem("v_evac", h), 1)

            def prepare(h):
                K, Q, XX = K_[h], Q_[h], X_[h]
                beta, a, n2, rt, rn, t_, d2, d3 = (sm[:, i, :] for i in range(8))
                K4 = K[:, :, :].rearrange("p (n i) d -> p n i d", i=C)
                Q4 = Q[:, :, :].rearrange("p (n i) d -> p n i d", i=C)
                X4 = XX[:, :, :].rearrange("p (n i) d -> p n i d", i=C)

                def at(v, i, j=None):
                    return v.rearrange("p (n i) -> p n i", i=C)[:, :, i:(j or i + 1)]

                def over(v, width):
                    return v.unsqueeze(2).broadcast_to([P, N, width])

                dve.wait_ge(sem("ksq"), h + 1)
                link(dve.tensor_reduce(n2, TMP[:, 0:N * HD].rearrange("p (t d) -> p t d", d=HD), AX_X, ALU.add))
                link(dve.tensor_scalar(n2, n2, K_EPS, None, ALU.add))
                rsqrt(n2, rt, rn, t_)
                dve.tensor_tensor(K[:, :, :], RAW[:, :, 1, :].rearrange("p d t -> p t d"), over(rn, HD), ALU.mult)\
                    .then_inc(sem("raw_used"), 1)
                dve.wait_ge(sem("ba_ready"), h + 1)
                link(dve.tensor_scalar(beta, beta, 2.0, None, ALU.mult))
                dve.tensor_tensor(XX[:, :, 0:HD], RAW[:, :, 2, :].rearrange("p d t -> p t d"), over(beta, HD), ALU.mult)\
                    .then_inc(sem("raw_used"), 1)
                dve.wait_ge(sem("q_raw", h), 1)
                dve.wait_ge(sem("raw_used"), 2 * h + 2)
                link(dve.tensor_tensor(at(d2, 1, C), at(a, 1, C), at(a, 0, C - 1), ALU.mult))
                link(dve.tensor_tensor(at(d3, 2, C), at(d2, 2, C), at(a, 0, C - 2), ALU.mult))
                decays = [None, a, d2, d3]
                Lf = L[:, :, :]
                for d in range(1, C):
                    T4 = TMP[:, 0:NCH * (C - d) * HD].rearrange("p (n i k) -> p n i k", n=NCH, i=C - d)
                    link(dve.tensor_tensor(T4, K4[:, :, d:C, :], K4[:, :, 0:C - d, :], ALU.mult))
                    diag = Lf[:, :, C * d:C * C:C + 1]
                    link(dve.tensor_reduce(diag, T4, AX_X, ALU.add))
                    w = at(t_, d, C)
                    link(dve.tensor_tensor(w, at(decays[d], d, C), at(beta, d, C), ALU.mult))
                    link(dve.tensor_tensor(diag, diag, w, ALU.mult))
                for d in range(C):
                    T4 = TMP[:, 0:NCH * (C - d) * HD].rearrange("p (n i k) -> p n i k", n=NCH, i=C - d)
                    link(dve.tensor_tensor(T4, Q4[:, :, d:C, :], K4[:, :, 0:C - d, :], ALU.mult))
                    w = at(PD[h][:, d, :], d, C)
                    link(dve.tensor_reduce(w, T4, AX_X, ALU.add))
                    if d:
                        link(dve.tensor_tensor(w, w, at(decays[d], d, C), ALU.mult))
                cs, ce = n2, rt
                link(dve.tensor_copy(at(cs, 0), at(a, 0)))
                for i in range(1, C):
                    link(dve.tensor_tensor(at(cs, i), at(cs, i - 1), at(a, i), ALU.mult))
                link(dve.memset(at(ce, C - 1), 1.0))
                for i in range(C - 2, -1, -1):
                    link(dve.tensor_tensor(at(ce, i), at(ce, i + 1), at(a, i + 1), ALU.mult))
                link(dve.tensor_copy(GAM[h][:, :].unsqueeze(2), at(cs, C - 1)))
                link(dve.tensor_tensor(t_, beta, cs, ALU.mult))
                link(dve.tensor_scalar(t_, t_, -1.0, None, ALU.mult))
                link(dve.tensor_tensor(XX[:, :, HD:2 * HD], K[:, :, :], over(t_, HD), ALU.mult))
                link(dve.tensor_tensor(K[:, :, :], K[:, :, :], over(ce, HD), ALU.mult))
                link(dve.tensor_tensor(Q[:, :, :], Q[:, :, :], over(cs, HD), ALU.mult))
                for j in range(C - 1):
                    m = C - 1 - j
                    T4 = TMP[:, 0:NCH * m * 2 * HD].rearrange("p (n i x) -> p n i x", n=NCH, i=m)
                    col = Lf[:, :, C * (j + 1) + j:C * C:C]
                    link(dve.tensor_tensor(T4, col.unsqueeze(3).broadcast_to([P, NCH, m, 2 * HD]),
                                           X4[:, :, j:j + 1, :].broadcast_to([P, NCH, m, 2 * HD]), ALU.mult))
                    ins = dve.tensor_tensor(X4[:, :, j + 1:C, :], X4[:, :, j + 1:C, :], T4, ALU.subtract)
                    if j < C - 2:
                        link(ins)
                    else:
                        ins.then_inc(sem("prep_done", h), 1)
                        dve.wait_ge(sem("prep_done", h), 1)

            def free_xn():
                dve.wait_ge(sem("xnt_ps"), PC)

            for pc in range(PC):
                values(0, pc)
            normalise(1, free_xn, "xn_ready")
            for pc in range(2):
                values(1, pc)
            prepare(0)
            for pc in range(2, PC):
                values(1, pc)
            prepare(1)

            for b in range(B):
                dve.wait_ge(sem("ga_ps"), b + 1)
                dve.scalar_tensor_tensor(out=WOG[:, b, :], in0=bank[5 + b % 2][:, 0:D], scalar=NW[:, 0:1], in1=WO[:, :],
                                         op0=ALU.mult, op1=ALU.mult).then_inc(sem("wog_ready"), 1)

            for h in range(NHALF):
                dve.memset(S_[h][:, 0, :, :], 0.0).then_inc(sem("s_ready", h), 1)

            def from_state(h, n):
                dve.wait_ge(sem("s_ready", h), n + 1)
                s_ = S_[h][:, n % SR, :, :].unsqueeze(1).broadcast_to([P, C, HD, HD])
                w = X_[h][:, n * C:(n + 1) * C, HD:2 * HD].unsqueeze(2).broadcast_to([P, C, HD, HD])
                dve.tensor_tensor(p1[h][:, n % UR, :, :, 0:HD], s_, w, ALU.mult).then_inc(sem("seq_w", h), 1)

            def sum_u(h, n):
                dve.wait_ge(sem("seq_w", h), n + 1)
                dve.wait_ge(sem("ubar_in", h), n // 2 + 1)
                dve.tensor_reduce(X_[h][:, n * C:(n + 1) * C, 0:HD], p1[h][:, n % UR, :, :, :], AX_X, ALU.add)\
                    .then_inc(sem("u_ready", h), 1)

            def outer(h, n):
                dve.wait_ge(sem("u_ready", h), n + 1)
                u = X_[h][:, n * C:(n + 1) * C, 0:HD].rearrange("p i v -> p v i").unsqueeze(2).broadcast_to([P, HD, HD, C])
                k = K_[h][:, n * C:(n + 1) * C, :].rearrange("p i k -> p k i").unsqueeze(1).broadcast_to([P, HD, HD, C])
                dve.tensor_tensor(p2[h][:, :, :, 0:C], u, k, ALU.mult).then_inc(sem("seq_k", h), 1)

            def next_state(h, n):
                dve.wait_ge(sem("seq_k", h), n + 1)
                dve.wait_ge(sem("decayed", h), n + 1)
                if n + 1 >= SR:
                    dve.wait_ge(sem("prod_ready", h), (n + 1 - SR) // GC + 1)
                dve.tensor_reduce(S_[h][:, (n + 1) % SR, :, :], p2[h][:, :, :, :], AX_X, ALU.add).then_inc(sem("s_ready", h), 1)

            for n in range(NCH):
                for step in (from_state, sum_u, outer, next_state):
                    if step in (outer, next_state) and n == NCH - 1:
                        continue
                    for h in range(NHALF):
                        step(h, n)

            for h in range(NHALF):
                ms, rt, rn, t_ = (sm[:, i, :] for i in (2, 3, 4, 5))
                dve.wait_ge(sem("sqo"), h + 1)
                dve.tensor_reduce(ms, SQO[:, :, :], AX_X, ALU.add).then_inc(sem("sqo_used"), 1)
                dve.wait_ge(sem("sqo_used"), h + 1)
                link(dve.tensor_scalar(ms, ms, 1.0 / HD, O_EPS, ALU.mult, ALU.add))
                rsqrt(ms, rt, rn, t_)
                dve.tensor_tensor(OV[h][:, :, :], K_[h][:, :, :].rearrange("p t v -> p v t"),
                                  rn.unsqueeze(1).broadcast_to([P, HD, N]), ALU.mult).then_inc(sem("ov_ready", h), 1)

            def attend(h):
                for q in range(4):
                    k = 4 * h + q
                    dve.wait_ge(sem("att_ps"), k + 1)
                    xr = X[:, 4 * k:4 * k + 4, :]
                    dve.tensor_tensor(xr, xr, bank[5 + k % 2][:, :].rearrange("p (n d) -> p n d", n=4), ALU.add)\
                        .then_inc(sem("x1_ready"), 1)
                dve.wait_ge(sem("x1_ready"), 4 * (h + 1))

            def route(h):
                l3 = [P, NT, E]
                dve.wait_ge(sem("lg_ps", h), PC)
                dve.tensor_tensor(lg[:, :, :], bank[1][:, 0:NT * E].rearrange("p (t e) -> p t e", e=E),
                                  RB[:, :].unsqueeze(1).broadcast_to(l3), ALU.add).then_inc(sem("lg_ready", h), 1)
                dve.wait_ge(sem("lg_ready", h), 1)
                link(dve.tensor_reduce(lmx[:, :], lg[:, :, :], AX_X, ALU.max))
                top = lmx[:, :].unsqueeze(2).broadcast_to(l3)
                dve.tensor_tensor(t8[:, :, :], lg[:, :, :], top, ALU.subtract).then_inc(sem("lsub"), 1)
                link(dve.tensor_tensor(oh[:, :, :], lg[:, :, :], top, ALU.is_equal))
                link(dve.tensor_tensor(oh[:, :, :], oh[:, :, :], rev[:, :].unsqueeze(1).broadcast_to(l3), ALU.mult))
                link(dve.tensor_reduce(lm[:, :], oh[:, :, :], AX_X, ALU.max))
                dve.tensor_tensor(oh[:, :, :], rev[:, :].unsqueeze(1).broadcast_to(l3), lm[:, :].unsqueeze(2).broadcast_to(l3), ALU.is_equal)\
                    .then_inc(sem("oh_ready", h), 1)
                dve.wait_ge(sem("lexp"), h + 1)
                link(dve.tensor_reduce(posf[:, :], t8[:, :, :], AX_X, ALU.add))
                link(dve.reciprocal(maxp[h][:, :], posf[:, :]))
                dve.wait_ge(sem("rank_ps", h), 1)
                link(dve.tensor_copy(tot[:, :, :], bank[4][:, 0:NT * E].rearrange("p (t e) -> p e t", e=E)))
                flat = "p e t -> p (e t)"
                link(dve.tensor_tensor_scan(exc[:, :, :].rearrange(flat), msk[:, :, :].rearrange(flat),
                                            tot[:, :, :].rearrange(flat), 0.0, ALU.mult, ALU.add))
                cnt = exc[:, :, NT - 1:NT]
                link(dve.tensor_tensor(cmn[:, :, :], cnt.broadcast_to([P, E, NT]), i128[:, :].unsqueeze(1).broadcast_to([P, E, NT]), ALU.is_gt))
                link(dve.tensor_reduce(nt8[:, :], cmn[:, :, :], AX_X, ALU.add))
                link(dve.tensor_tensor_scan(cu8[:, :], one8[:, :], nt8[:, :], 0.0, ALU.mult, ALU.add))
                link(dve.tensor_tensor(ba8[:, :], cu8[:, :], nt8[:, :], ALU.subtract))
                link(dve.tensor_scalar(ba8[:, :], ba8[:, :], float(P), None, ALU.mult))
                link(dve.tensor_tensor(cmp[:, :, :], ij[:, :].unsqueeze(2).broadcast_to([P, NF, E]),
                                       cu8[:, :].unsqueeze(1).broadcast_to([P, NF, E]), ALU.is_ge))
                link(dve.tensor_reduce(texf[:, :], cmp[:, :, :], AX_X, ALU.add))
                dve.tensor_scalar(tex[h][:, :], texf[:, :], float(E - 1), None, ALU.min).then_inc(sem("tex_ready", h), 1)
                link(dve.tensor_tensor(exc[:, :, :], exc[:, :, :], tot[:, :, :], ALU.subtract))
                link(dve.tensor_tensor(exc[:, :, :], exc[:, :, :], ba8[:, :].unsqueeze(2).broadcast_to([P, E, NT]), ALU.add))
                link(dve.tensor_tensor(t8[:, :, :], exc[:, :, :].rearrange("p e t -> p t e"),
                                       bank[3][:, 0:NT * E].rearrange("p (t e) -> p t e", e=E), ALU.add))
                link(dve.tensor_tensor(t8[:, :, :], t8[:, :, :], oh[:, :, :], ALU.mult))
                link(dve.tensor_reduce(posf[:, :], t8[:, :, :], AX_X, ALU.add))
                dve.tensor_copy(pos[h][:, :], posf[:, :]).then_inc(sem("pos_ready", h), 1)
                dve.wait_ge(sem("pos_ready", h), 1)

            for h in range(NHALF):
                attend(h)
            for h in range(NHALF):
                def free2(h=h):
                    if h == 1:
                        dve.wait_ge(sem("xn2t_ps"), PC)
                normalise(h, free2, "xn2_ready")
                route(h)

            G = NHALF * NF

            def xst(g):
                dve.wait_ge(sem("xs_used"), g + 1)
                if g >= 2:
                    dve.wait_ge(sem("h_ps"), 2 * (g - 1))
                dve.tensor_copy(XST[:, g % 2, :], bank[0][:, 0:P]).then_inc(sem("xst_ready"), 1)

            def gate_u(g):
                dve.wait_ge(sem("silu_a"), g + 1)
                dve.wait_ge(sem("h_ps"), 2 * g + 2)
                dve.tensor_tensor(GU[:, g % 2, :], GU[:, g % 2, :], bank[(2, 7)[g % 2]][:, :], ALU.mult)\
                    .then_inc(sem("gu_ready"), 1)

            def ys(g):
                dve.wait_ge(sem("y_ps"), g + 1)
                if g >= 4:
                    dve.wait_ge(sem(f"ys_out{g % 4}_", (g - 4) // NF), 16 * stores(g - 4))
                dve.tensor_copy(YS[:, g % 4, :], bank[4][:, 0:D]).then_inc(sem("ys_ready"), 1)

            xst(0)
            for g in range(G + 2):
                if g + 1 < G:
                    xst(g + 1)
                if g < G:
                    gate_u(g)
                if g >= 2:
                    ys(g - 2)

            for h in range(NHALF):
                for q in range(4):
                    dve.wait_ge(sem("gathered", h), 16 * NT)
                    for b2 in range(2):
                        b = h * HB + 2 * q + b2
                        dve.wait_ge(sem("gb_ps"), b + 1)
                        for s in range(2):
                            t = 4 * q + 2 * b2 + s
                            last = dve.scalar_tensor_tensor(out=YG[h][:, t, :], in0=YG[h][:, t, :], scalar=maxp[h][:, t:t + 1],
                                                            in1=bank[5 + b % 2][:, 0:D], op0=ALU.mult, op1=ALU.mult)
                        last.then_inc(sem("gb_used"), 1)
                    dve.wait_ge(sem("gb_used"), h * HB + 2 * q + 2)
                    t0 = h * NT + 4 * q
                    dve.tensor_tensor(X[:, t0:t0 + 4, :], X[:, t0:t0 + 4, :], YG[h][:, 4 * q:4 * q + 4, :], ALU.add)\
                        .then_inc(sem("out_ready", h), 1)


_INS = ["L0_attn_x", "L0_attn_Wq", "L0_attn_Wk", "L0_attn_Wv", "L0_attn_Wo", "L0_attn_Wbet", "L0_attn_Wf", "L0_attn_norm_w",
        "L0_ffn_router_w", "L0_ffn_router_b", "L0_ffn_w1", "L0_ffn_w2", "L0_c", "L0_wmod"]
_OUTS = [((16, 256, 128), "float32")]


def kernel(**inputs):
    import numpy as _np
    import concourse.bacc as _bacc
    from concourse import mybir as _mybir
    from concourse.bass_utils import run_bass_kernel_spmd as _run

    nc = _bacc.Bacc("TRN2", target_bir_lowering=False, num_devices=1)
    arrays, args = {}, []
    for name in _INS:
        a = _np.ascontiguousarray(inputs[name])
        arrays[f"in_{name}_dram"] = a
        args.append(nc.dram_tensor(f"in_{name}_dram", a.shape, _mybir.dt.from_np(a.dtype), kind="ExternalInput").ap())
    for i, (shape, dtype) in enumerate(_OUTS):
        dt = _mybir.dt.from_np(_np.dtype(dtype))
        args.append(nc.dram_tensor(f"out_{i}_dram", shape, dt, kind="ExternalOutput").ap())
    adaln_block(nc, *args)
    r = _run(nc, [arrays], core_ids=[0])
    got = tuple(r.results[0][f"out_{i}_dram"] for i in range(len(_OUTS)))
    return got[0]
```

```python
from contextlib import ExitStack

import concourse.bass as bass
from concourse import mybir

F32 = mybir.dt.float32
I32 = mybir.dt.int32
U32 = mybir.dt.uint32
ALU = mybir.AluOpType
ACT = mybir.ActivationFunctionType
AX_X = mybir.AxisListType.X

P = 128
LN_EPS = 1e-5
K_EPS = 1e-12
O_EPS = 1e-6


def adaln_block(nc, x, Wq, Wk, Wv, Wo, Wbet, Wf, norm_w, router_w, router_b, w1, w2, c, wmod, out):
    B, N, D = x.shape
    H = Wbet.shape[1]
    HD = D // H
    E, _, F2 = w1.shape
    FF = F2 // 2
    FC = FF // P
    NHALF = 2
    HB = B // NHALF
    NTIME = N // P
    assert HB * H == P and N == 2 * P and D == P
    NT = HB * N // P
    PC = 4
    CT = NT // PC
    C = 4
    NCH = N // C
    GC = 4
    NG = NCH // GC
    SR = 16
    UR = 4
    NS = HD + C
    XR = 7
    YR = 8
    PG = NG - 1
    AT_SQUARES = (NG // 2 + 1) * GC + GC - 1
    AT_SUMS, AT_ROOTS, AT_ATTEND, AT_STATS, AT_ROWS = AT_SQUARES + 2, AT_SQUARES + 4, 50, 51, 55
    F_ATTEND, F_ROOT, F_TURN, F_GATES = 3, 8, 9, 15
    MOVE = 4
    SCAT = F_TURN + 3
    YIN = 12
    NF = NT + E - 1
    NFE = NF * P

    D1 = D + 1
    sorted_h = [nc.dram_tensor(f"sorted_h{s}", (NFE, D1), F32, kind="Internal").ap() for s in range(NTIME)]
    placed_y = [nc.dram_tensor(f"placed_y{s}", (NT * P + NFE, D), F32, kind="Internal").ap() for s in range(NTIME)]
    x_t = x.rearrange("b (s p) d -> p (b s) d", p=P)
    out_t = out.rearrange("b (s p) d -> s p b d", p=P)

    with ExitStack() as ctx:
        def sb(name, shape, dt=F32):
            return ctx.enter_context(nc.sbuf_tensor(name, shape, dt))

        sems = {}

        def sem(name, h=None):
            key = name if h is None else f"{name}{h}"
            if key not in sems:
                sems[key] = ctx.enter_context(nc.semaphore(key))
            return sems[key]

        X = sb("X", [P, B * N // P, D])
        XNB = sb("XN", [P, NT, D])
        big = sb("big", [P, 12288])
        RAW = big[:, 0:6144].rearrange("p (d x t) -> p d x t", d=HD, x=3)
        TMP = big[:, 6144:9216]
        QKV = big[:, 9216:12288].rearrange("p (r b x t) -> p r b x t", r=2, b=2, x=3)
        W1 = big[:, 0:E * F2].rearrange("p (e f) -> p e f", e=E)
        W2 = big[:, E * F2:12288].rearrange("p (e c d) -> p e c d", e=E, c=FC)
        ph = sb("ph", [P, 2048])
        HT = ph[:, 0:1024].rearrange("p (r t) -> p r t", r=2)
        BFT = ph[:, 1024:2048].rearrange("p (r b t) -> p r b t", r=2, b=2)
        WOG = ph[:, :].rearrange("p (b d) -> p b d", b=B)
        WP = sb("WP", [P, 3, D])
        WBF = sb("WBF", [P, H, 2])
        WBFR = sb("WBFR", [P, 2, H])
        WO = sb("WO", [P, D])
        NW = sb("NW", [P, 1])
        RW = sb("RW", [P, E])
        RB = sb("RB", [P, E])
        CT_ = sb("CT_", [P, B])
        MOD = sb("MOD", [P, 4, B])
        GATE = sb("GATE", [B, 2, D])
        ID = sb("ID", [P, P])
        LOWER = sb("LOWER", [P, P])
        ONES = sb("ONES", [P, P])
        prod_o = sb("prod_o", [P, 2, NS, GC * C * HD])
        K_ = [sb(f"K{h}", [P, N, HD]) for h in range(NHALF)]
        Q_ = [sb(f"Q{h}", [P, N, HD]) for h in range(NHALF)]
        X_ = [sb(f"X{h}", [P, N, 2 * HD]) for h in range(NHALF)]
        PD = [sb(f"PD{h}", [P, C, N]) for h in range(NHALF)]
        GAM = [sb(f"GAM{h}", [P, NCH]) for h in range(NHALF)]
        S_ = [sb(f"S{h}", [P, SR, HD, HD]) for h in range(NHALF)]
        p1 = [sb(f"p1{h}", [P, UR, C, HD, HD + 1]) for h in range(NHALF)]
        p2 = [sb(f"p2{h}", [P, HD, HD, C + 1]) for h in range(NHALF)]
        sm = sb("sm", [P, 8, N])
        st = sb("st", [P, NT, 6])
        mv = sb("mv", [P, NT, 2])
        ve = sb("ve", [P, NT])
        sd = sb("sd", [P, NT])
        yy = sb("yy", [P, NT])
        y2 = sb("y2", [P, NT])
        lg = sb("lg", [P, NT, E])
        lm = sb("lm", [P, NT])
        lmx = sb("lmx", [P, NT])
        oh = sb("oh", [P, NT, E])
        t8 = sb("t8", [P, NT, E])
        tot = sb("tot", [P, E, NT])
        exc = sb("exc", [P, E, NT])
        msk = sb("msk", [P, E, NT])
        rev = sb("rev", [P, E])
        i128 = sb("i128", [P, NT])
        ij = sb("ij", [P, NF])
        one8 = sb("one8", [P, E])
        nt8 = sb("nt8", [P, E])
        cu8 = sb("cu8", [P, E])
        ba8 = sb("ba8", [P, E])
        cmp = sb("cmp", [P, NF, E])
        cmn = sb("cmn", [P, E, NT])
        ex = sb("ex", [P, NT, E])
        texf = sb("texf", [P, NF])
        posf = sb("posf", [P, NT])
        place = sb("place", [P, 2 * NF], U32)
        maxp = [sb(f"maxp{h}", [P, NT]) for h in range(NHALF)]
        tex = [sb(f"tex{h}", [P, NF], I32) for h in range(NHALF)]
        pos = [sb(f"pos{h}", [P, NT], U32) for h in range(NHALF)]

        bank = [ctx.enter_context(nc.psum_tensor(f"bank{i}", [P, 512], F32)) for i in range(8)]

        ATT_BANKS = [[bank[i] for i in (4, 5, 0, 1)], [bank[i] for i in (4, 5, 4, 5)]]
        TURN_BANKS = [[bank[i] for i in (0, 1, 0, 1)], [bank[4]] * 4]
        BACK_BANKS = [[bank[i] for i in (2, 3, 2, 3)], [bank[5]] * 4]

        block = ctx.enter_context(nc.Block())

        k1 = K_[1][:, :, :].rearrange("p t d -> p (t d)")
        WM = k1[:, 0:6 * D].rearrange("p (j f) -> p j f", j=6)
        CROW = k1[0:B, 6 * D:7 * D]
        CE = k1[0:B, 7 * D:8 * D]
        GTMP = k1[0:B, 8 * D:10 * D].rearrange("p (j d) -> p j d", j=2)
        po1 = prod_o[:, 1, :, :].rearrange("p a b -> p (a b)")
        L = po1[:, 0:NCH * C * C].rearrange("p (n a) -> p n a", n=NCH)
        BA = po1[:, NCH * C * C:NCH * C * C + 2 * N].rearrange("p (x t) -> p x t", x=2)
        OT = [X_[h][:, 0:P // 2, :].rearrange("p t d -> p (t d)").rearrange("p (b t) -> p b t", b=HB) for h in range(NHALF)]
        flatx = [X_[h][:, :, :].rearrange("p t d -> p (t d)") for h in range(NHALF)]
        H2 = [[flatx[h][:, HB * P + s * HB * D1:HB * P + (s + 1) * HB * D1].rearrange("p (n d) -> p n d", d=D1)
               for h in range(NHALF)] for s in range(NTIME)]
        YG = [[K_[h][:, s * P:(s + 1) * P, :].rearrange("p t d -> p (t d)").rearrange("p (n d) -> p n d", n=HB)
               for h in range(NHALF)] for s in range(NTIME)]
        OV = [[Q_[h][:, s * P:(s + 1) * P, :].rearrange("p t d -> p (t d)").rearrange("p (v t) -> p v t", v=HD)
               for h in range(NHALF)] for s in range(NTIME)]
        XG = [X[:, :, :].rearrange("p (b s) d -> p s b d", s=NTIME)[:, s, :, :] for s in range(NTIME)]
        XN1 = X_[1][:, 0:P, :].rearrange("p t d -> p (t d)").rearrange("p (n d) -> p n d", n=NT)
        XN = [XNB[:, :, :], XN1]
        SM = [sm, XNB[:, :, :].rearrange("p n d -> p (n d)").rearrange("p (x t) -> p x t", x=8)]
        SQO = [[XNB[:, h * HB:(h + 1) * HB, :].rearrange("p n d -> p (n d)").rearrange("p (t v) -> p t v", v=HD) for h in range(NHALF)],
               [flatx[h][:, HB * P + HB * D1:2 * HB * P + HB * D1].rearrange("p (t v) -> p t v", v=HD) for h in range(NHALF)]]
        flatq = [Q_[h][:, :, :].rearrange("p t d -> p (t d)") for h in range(NHALF)]
        XS = flatq[0][:, 0:XR * D1].rearrange("p (r d) -> p r d", r=XR)
        XST = flatq[1][:, 0:2 * P].rearrange("p (r d) -> p r d", r=2)
        YS = flatq[1][:, 2 * P:2 * P + YR * D].rearrange("p (r d) -> p r d", r=YR)
        GU, GUT = (S_[h][:, :, :, :].rearrange("p n v k -> p (n v k)").rearrange("p (r f) -> p r f", r=2) for h in range(NHALF))
        GB = WOG
        QK = prod_o[:, 0, :, :].rearrange("p a b -> p (a b)")
        PADS = TMP[:, 0:NF * D1].rearrange("p (n d) -> p n d", n=NF)
        H2T = K_[0][:, 0:P, :].rearrange("p t d -> p (t d)").rearrange("p (r t) -> p r t", r=2)

        def scale_outputs(engine, s):
            rn = sm[:, 4, :]
            for h in range(NHALF):
                engine.wait_ge(sem("prod_ready", h), (s + 1) * NG // 2)
                engine.tensor_tensor(OV[s][h], K_[h][:, s * P:(s + 1) * P, :].rearrange("p t v -> p v t"),
                                     rn[:, h * P:(h + 1) * P].unsqueeze(1).broadcast_to([P, HD, P]), ALU.mult)\
                    .then_inc(sem(f"ov_ready{h}_", s), 1)

        def move_outputs(queue, s):
            for h in range(NHALF):
                queue.wait_ge(sem(f"ov_ready{h}_", s), 1)
                if s == 0:
                    queue.wait_ge(sem("prod_ready", h), NG // 2)
                else:
                    queue.wait_ge(sem("att_ps", 0), 4)
                for b in range(HB):
                    queue.dma_start(OT[h][:, b, :], OV[s][h][b * H:(b + 1) * H, :, :]).then_inc(sem(f"ot_in{h}_", s), 16)

        def make_products(engine, g, h):
            k = g * NHALF + h
            if k >= 2:
                engine.wait_ge(sem("o_ps"), k - 1)
            elif k == 0:
                for hh in range(NHALF):
                    engine.wait_ge(sem("prep_done", hh), 1)
            slot = prod_o[:, k % 2, :, :].rearrange("p s (n i v) -> p s n i v", n=GC, i=C)
            for m in range(GC):
                n = g * GC + m
                engine.wait_ge(sem("s_ready", h), n + 1)
                q = Q_[h][:, n * C:(n + 1) * C, :].rearrange("p i k -> p k i").unsqueeze(3).broadcast_to([P, HD, C, HD])
                s_ = S_[h][:, n % SR, :, :].rearrange("p v k -> p k v").unsqueeze(2).broadcast_to([P, HD, C, HD])
                engine.tensor_tensor(slot[:, 0:HD, m, :, :], q, s_, ALU.mult)
            engine.wait_ge(sem("u_ready", h), (g + 1) * GC)
            u = X_[h][:, :, 0:HD].rearrange("p (n i) v -> p n i v", i=C)[:, g * GC:(g + 1) * GC, :, :]
            for d in range(C):
                w = PD[h][:, d, :].rearrange("p (n i) -> p n i", i=C)[:, g * GC:(g + 1) * GC, d:C]
                last = engine.tensor_tensor(slot[:, HD + d, :, d:C, :], w.unsqueeze(3).broadcast_to([P, GC, C - d, HD]),
                                            u[:, :, 0:C - d, :], ALU.mult)
            last.then_inc(sem("prod_ready", h), 1)

        def load_y(queue, s, q):
            if q == 0:
                for g in range((s + 1) * NF - YR, (s + 1) * NF):
                    queue.wait_ge(sem(f"ys_out{g % YR}"), 16 * (g // YR + 1))
            rows = placed_y[s][4 * q * P:4 * (q + 1) * P, :].rearrange("(n p) d -> p n d", p=P)
            queue.dma_start(YG[s][q // 2][:, q % 2 * 4:q % 2 * 4 + 4, :], rows).then_inc(sem(f"y_in{q}"), 16)

        def store_out(queue, s, q):
            queue.wait_ge(sem("out_ready", s), q + 1)
            queue.dma_start(out_t[s][:, 4 * q:4 * q + 4, :], XG[s][:, 4 * q:4 * q + 4, :]).then_inc(sem("stored"), 16)

        def shifted(queue, k):
            queue.wait_ge(sem("shifted"), 4 * (k + 1))

        def over(v):
            return v.unsqueeze(2).broadcast_to([P, N, HD])

        @block.sync
        def _(sp):
            sp.dma_start(CROW[:, :], c).then_inc(sem("c_in"), 16)
            sp.dma_start(WM[:, :, :], wmod.rearrange("d (j f) -> d j f", j=6)).then_inc(sem("wm_in"), 16)
            for i in range(4):
                sp.dma_start(X[:, 4 * i:4 * i + 4, :], x_t[:, 4 * i:4 * i + 4, :]).then_inc(sem(f"x_in{i}"), 16)
            for i, w in enumerate((Wq, Wk, Wv)):
                sp.dma_start(WP[:, i, :], w).then_inc(sem("w_in"), 16)
            sp.dma_start(WBFR[:, 0, :], Wbet).then_inc(sem("w_in"), 16)
            sp.dma_start(WBFR[:, 1, :], Wf).then_inc(sem("w_in"), 16)
            for i in range(4, 8):
                sp.dma_start(X[:, 4 * i:4 * i + 4, :], x_t[:, 4 * i:4 * i + 4, :]).then_inc(sem(f"x_in{i}"), 16)
            sp.dma_start(WO[:, :], Wo).then_inc(sem("wo_in"), 16)
            sp.dma_start(NW[:, :], norm_w.rearrange("(p a) -> p a", a=1)).then_inc(sem("wo_in"), 16)
            sp.dma_start(RW[:, :], router_w).then_inc(sem("wo_in"), 16)
            sp.dma_start(RB[:, :], router_b.rearrange("(a e) -> a e", a=1).broadcast_to([P, E])).then_inc(sem("wo_in"), 16)
            sp.wait_ge(sem("const_set"), 1)
            for s in range(NTIME):
                sp.dma_start(sorted_h[s].rearrange("(n p) d -> p n d", p=P), PADS[:, :, :]).then_inc(sem("padded", s), 16)

            for h in range(NHALF):
                for pc in range(PC):
                    for b2 in range(2):
                        b = 2 * pc + b2
                        if b2 == 0:
                            sp.wait_ge(sem("proj_evac", h), 4 * (pc + 1))
                        if h == 1 and pc == 0 and b2 == 0:
                            sp.wait_ge(sem("q_raw", 0), 1)
                            sp.wait_ge(sem("raw_used"), 1)
                            sp.wait_ge(sem("uw_started", 0), 1)
                        r = pc % 2
                        sp.dma_start(RAW[b * H:(b + 1) * H, :, :, :], QKV[:, r, b2, :, :]).then_inc(sem(f"raw_in{r}_", h), 16)
                        sp.dma_start(BA[b * H:(b + 1) * H, :, :], BFT[0:2 * H, r, b2, :]).then_inc(sem(f"raw_in{r}_", h), 16)
            sp.wait_ge(sem("prep_done", 1), 1)
            sp.dma_start(W1, w1.rearrange("e d f -> d e f")).then_inc(sem("w1_in"), 16)
            sp.dma_start(W2, w2.rearrange("e (c p) d -> p e c d", p=P)).then_inc(sem("w2_in"), 16)
            move_outputs(sp, 0)
            for g in range(NTIME * NF):
                s, j = divmod(g, NF)
                if j == 0:
                    sp.wait_ge(sem("scattered", s), 16 * NT)
                if g >= XR:
                    sp.wait_ge(sem("xst_ready"), g - XR + 1)
                    sp.wait_ge(sem("place_ready"), g - XR + 1)
                sp.dma_start(XS[:, g % XR, :], sorted_h[s][j * P:(j + 1) * P, :]).then_inc(sem(f"xs_in{g % XR}"), 16)
                if g == MOVE:
                    move_outputs(sp, 1)
                if NF + YIN <= g < NF + YIN + 4:
                    load_y(sp, 0, g - NF - YIN)
                if NF + YIN + 4 <= g < NF + YIN + 8:
                    store_out(sp, 0, g - NF - YIN - 4)
            for q in range(4):
                load_y(sp, 1, q)
            for q in range(4):
                store_out(sp, 1, q)
            sp.wait_ge(sem("stored"), 16 * 8)

        @block.tensor
        def _(pe):
            pe.wait_ge(sem("const_set"), 1)
            pe.wait_ge(sem("ce_ready"), 1)
            pe.transpose(bank[0][:, 0:B], CE[:, :], ID[0:B, 0:B]).then_inc(sem("ct_ps"), 1)
            pe.wait_ge(sem("ct_ready"), 1)
            pe.wait_ge(sem("wm_in"), 16)
            for i, j in enumerate((0, 1, 3, 4)):
                m = pe.matmul(bank[1][:, i * B:(i + 1) * B], WM[:, j, :], CT_[:, :], start=True, stop=True)
            m.then_inc(sem("mod_ps"), 1)
            for i, j in enumerate((2, 5)):
                m = pe.matmul(bank[5][0:B, i * D:(i + 1) * D], CT_[:, :], WM[:, j, :], start=True, stop=True)
            m.then_inc(sem("gate_ps"), 1)

            def turn_rows(k):
                h, pc = divmod(k, PC)
                pe.wait_ge(sem("xn_ready", h), CT * (pc + 1))
                if k >= 2:
                    pe.wait_ge(sem("ht_evac"), 2 * (k - 1))
                elif k == 0:
                    pe.wait_ge(sem("ct_ready"), 1)
                for i in range(CT):
                    m = pe.transpose(bank[(0, 7)[k % 2]][:, i * P:(i + 1) * P], XN[h][:, pc * CT + i, :], ID[:, :])
                m.then_inc(sem("xnt_ps"), 1)

            def project(k):
                pe.wait_ge(sem("ht_evac"), 2 * (k + 1))
                if k == 0:
                    pe.wait_ge(sem("w_in"), 16 * 5)
                    pe.wait_ge(sem("wbf_ready"), 1)
                    pe.wait_ge(sem("mod_ready"), 3)
                rhs = HT[:, k % 2, :]
                for i in range(3):
                    if k >= 1:
                        pe.wait_ge(sem("proj_evac", (k - 1) // PC), 4 * ((k - 1) % PC) + i + 1)
                    pe.matmul(bank[1 + i][:, :], WP[:, i, :], rhs, start=True, stop=True).then_inc(sem("proj_ps"), 1)
                if k >= 1:
                    pe.wait_ge(sem("proj_evac", (k - 1) // PC), 4 * ((k - 1) % PC) + 4)
                pe.matmul(bank[4][0:2 * H, :], WBF[:, :, :].rearrange("p h x -> p (h x)"), rhs, start=True, stop=True)\
                    .then_inc(sem("proj_ps"), 1)

            turn_rows(0)
            for k in range(NHALF * PC):
                if k + 1 < NHALF * PC:
                    turn_rows(k + 1)
                project(k)

            for b in range(B):
                if b == 0:
                    pe.wait_ge(sem("ht_evac"), 2 * NHALF * PC)
                    pe.wait_ge(sem("gate_ready"), 1)
                m = pe.matmul(bank[(5, 6, 0, 7)[b // 4]][:, b % 4 * D:(b % 4 + 1) * D], ID[0:B, b:b + 1].broadcast_to([B, P]), GATE[:, 0, :],
                              start=True, stop=True)
                if b % 4 == 3:
                    m.then_inc(sem("ga_ps"), 1)

            def sum_outputs(g, h):
                k = g * NHALF + h
                pe.wait_ge(sem("prod_ready", h), g + 1)
                if k >= 2:
                    pe.wait_ge(sem("o_evac"), k - 1)
                ps = bank[6 + k % 2][:, 0:GC * C * HD]
                for i in range(HD):
                    pe.matmul(ps, ID[:, :], prod_o[:, k % 2, i, :], start=(i == 0), stop=False, skip_group_check=True)
                for d in range(C):
                    o4 = ps.rearrange("p (n i v) -> p n i v", n=GC, i=C)[:, :, d:C, :]
                    r4 = prod_o[:, k % 2, HD + d, :].rearrange("p (n i v) -> p n i v", n=GC, i=C)[:, :, d:C, :]
                    m = pe.matmul(o4, ID[:, :], r4, start=False, stop=(d == C - 1), skip_group_check=True)
                m.then_inc(sem("o_ps"), 1)

            def attend(s, q):
                h = q // 2
                if q % 2 == 0:
                    pe.wait_ge(sem(f"ot_in{h}_", s), 16 * HB)
                if s == 1 and q == 0:
                    pe.wait_ge(sem("pos_ready", 0), 1)
                    pe.wait_ge(sem("lg_ready", 0), 1)
                if s == 1 and q >= 2:
                    pe.wait_ge(sem("x1_ready", 1), q - 1)
                for i in range(4):
                    b = 4 * q + i
                    m = pe.matmul(ATT_BANKS[s][q][:, i * P:(i + 1) * P], OT[h][:, b % HB, :], WOG[:, b, :], start=True, stop=True)
                m.then_inc(sem("att_ps", s), 1)

            def turn_rows2(k):
                s, q = divmod(k, 4)
                pe.wait_ge(sem("xn2_ready", s), 4 * (q + 1))
                if s == 0 and q >= 2:
                    shifted(pe, k - 2)
                elif s == 1 and q >= 1:
                    pe.wait_ge(sem("lg_part"), q)
                for i in range(4):
                    m = pe.transpose(TURN_BANKS[s][q][:, i * P:(i + 1) * P], XNB[:, 4 * q + i, :], ID[:, :])
                m.then_inc(sem("xn2t_ps"), 1)

            def router(k):
                s, q = divmod(k, 4)
                shifted(pe, k)
                for i in range(4):
                    t = i if s else 4 * q + i
                    m = pe.matmul(bank[4 if s else 5][:, t * E:(t + 1) * E], H2T[:, k % 2, i * P:(i + 1) * P], RW[:, :], start=True, stop=True)
                m.then_inc(sem("lg_ps", s), 1)
                if k == 4:
                    pe.wait_ge(sem("x1_ready", 1), 4)
                elif k >= 2:
                    pe.wait_ge(sem("h2_evac"), k if s else k - 1)
                for i in range(4):
                    m = pe.transpose(BACK_BANKS[s][q][:, i * P:(i + 1) * P], H2T[:, k % 2, i * P:(i + 1) * P], ID[:, :])
                m.then_inc(sem("h2_ps"), 1)

            def gate_rows(q):
                if q == 0:
                    pe.wait_ge(sem("h2_evac"), 8)
                else:
                    pe.wait_ge(sem("gb_evac"), q)
                for i in range(4):
                    b = 4 * q + i
                    m = pe.matmul(bank[5][:, i * P:(i + 1) * P], ID[0:B, b:b + 1].broadcast_to([B, P]), GATE[:, 1, :], start=True, stop=True)
                m.then_inc(sem("gb_ps"), 1)

            def rank(s):
                pe.wait_ge(sem("oh_ready", s), 1)
                ohf = oh[:, :, :].rearrange("p t e -> p (t e)")
                pe.matmul(bank[4][:, 0:NT * E], LOWER[:, :], ohf, start=True, stop=True)
                pe.matmul(bank[4][:, NT * E:2 * NT * E], ONES[:, :], ohf, start=True, stop=True).then_inc(sem("rank_ps", s), 1)

            for g in range(NG):
                if g == AT_ATTEND // GC - 1:
                    pe.wait_ge(sem("wog_ready"), B)
                    for q in range(4):
                        attend(0, q)
                if g == AT_ROWS // GC:
                    turn_rows2(0)
                    for q in range(4):
                        if q < 3:
                            turn_rows2(q + 1)
                        router(q)
                for h in range(NHALF):
                    sum_outputs(g, h)
                    if g == AT_ROWS // GC and h == 0:
                        rank(0)

            pe.wait_ge(sem("w1_in"), 16)
            pe.wait_ge(sem("w2_in"), 16)
            pe.wait_ge(sem("h2_evac"), 4)
            pe.wait_ge(sem("o_evac"), NG * NHALF)
            G = NTIME * NF
            expert = {}

            def turn_x(g):
                pe.wait_ge(sem(f"xs_in{g % XR}"), 16 * (g // XR + 1))
                if g >= 1:
                    pe.wait_ge(sem("xst_ready"), g)
                if g >= 4:
                    pe.wait_ge(sem("ys_ready"), g - 3)
                pe.transpose(bank[0][:, 0:P], XS[:, g % XR, 0:D], ID[:, :]).then_inc(sem("xt_ps"), 1)

            def hidden(g):
                s, j = divmod(g, NF)
                if j == 0:
                    pe.wait_ge(sem("tex_ready", s), 1)
                expert[g] = pe.value_load(tex[s][0:1, j:j + 1], min_val=0, max_val=E - 1)
                pe.wait_ge(sem("xst_ready"), g + 1)
                for k in range(2):
                    if g >= 2:
                        pe.wait_ge(sem("silu_a") if k == 0 else sem("gu_ready"), g - 1)
                    pe.matmul(bank[(1, 6)[g % 2] + k][:, :], XST[:, g % 2, :],
                              W1[:, bass.ds(expert[g], 1), k * FF:(k + 1) * FF],
                              start=True, stop=True).then_inc(sem("h_ps"), 1)
                    if k == 0 and g + 1 < G:
                        turn_x(g + 1)

            def turn_g(g):
                pe.wait_ge(sem("gu_ready"), g + 1)
                if g >= 1:
                    pe.wait_ge(sem("gut_ready"), g)
                for k in range(FC):
                    m = pe.transpose(bank[3][:, k * P:(k + 1) * P], GU[:, g % 2, k * P:(k + 1) * P], ID[:, :])
                m.then_inc(sem("gut_ps"), 1)

            def second(g):
                pe.wait_ge(sem("gut_ready"), g + 1)
                if g >= 1:
                    pe.wait_ge(sem("ys_ready"), g)
                pe.wait_ge(sem("xst_ready"), min(g + 4, G))
                for k in range(FC):
                    m = pe.matmul(bank[0][:, P:P + D], GUT[:, g % 2, k * P:(k + 1) * P], W2[:, bass.ds(expert[g], 1), k, :],
                                  start=(k == 0), stop=(k == FC - 1))
                m.then_inc(sem("y_ps"), 1)

            turn_x(0)
            for g in range(G + 2):
                if g < G:
                    hidden(g)
                if F_TURN <= g < F_TURN + 4:
                    turn_rows2(g - F_TURN + 4)
                if 0 <= g - 1 < G:
                    turn_g(g - 1)
                if g >= 2:
                    second(g - 2)
                if g in (F_ATTEND, F_ATTEND + 2):
                    for q in (g - F_ATTEND, g - F_ATTEND + 1):
                        attend(1, q)
                if F_GATES <= g < F_GATES + 4:
                    gate_rows(g - F_GATES)
                if F_TURN <= g < F_TURN + 4:
                    router(g - F_TURN + 4)
                if g == F_TURN + 5:
                    rank(1)

        @block.gpsimd
        def _(pool):
            done = [0]

            def link(ins):
                done[0] += 1
                ins.then_inc(sem("pool_link"), 1)
                pool.wait_ge(sem("pool_link"), done[0])

            pool.memset(ID[:, :], 0.0)
            pool.memset(LOWER[:, :], 1.0)
            pool.memset(ONES[:, :], 1.0)
            pool.memset(PADS[:, :, :], 0.0)
            pool.memset(one8[:, :], 1.0)
            link(pool.memset(msk[:, :, :], 1.0))
            pool.affine_select(out=ID[:, :], in_=ID[:, :], compare_op=ALU.not_equal, fill=1.0, base=0,
                               pattern=[[-1, P]], channel_multiplier=1)
            pool.affine_select(out=LOWER[:, :], in_=LOWER[:, :], compare_op=ALU.is_gt, fill=0.0, base=0,
                               pattern=[[1, P]], channel_multiplier=-1)
            pool.memset(msk[:, :, 0:1], 0.0)
            pool.iota(rev[:, :], [[-1, E]], base=E, channel_multiplier=0, allow_small_or_imprecise_dtypes=True)
            pool.iota(i128[:, :], [[P, NT]], base=0, channel_multiplier=0, allow_small_or_imprecise_dtypes=True)
            pool.iota(PADS[:, :, D:D1], [[P, NF], [0, 1]], base=NT * P, channel_multiplier=1, allow_small_or_imprecise_dtypes=True)
            pool.iota(ij[:, :], [[1, NF]], base=0, channel_multiplier=0, allow_small_or_imprecise_dtypes=True)\
                .then_inc(sem("const_set"), 1)

            for h in range(NHALF):
                beta, cs, ce, w = (SM[h][:, i, :] for i in (0, 2, 3, 4))
                pool.wait_ge(sem("beta_ready", h), 1)
                if h == 1:
                    pool.wait_ge(sem("xnt_ps"), NHALF * PC)
                pool.tensor_tensor(X_[h][:, :, 0:HD], RAW[:, :, 2, :].rearrange("p d t -> p t d"), over(beta), ALU.mult)\
                    .then_inc(sem("uw_started", h), 1)
                pool.wait_ge(sem("decays_ready", h), 1)
                pool.tensor_tensor(X_[h][:, :, HD:2 * HD], K_[h][:, :, :], over(w), ALU.mult).then_inc(sem("uw_started", h), 1)
                pool.wait_ge(sem("uw_started", h), 2)
                pool.wait_ge(sem("q_raw", h), 1)
                K4 = K_[h][:, :, :].rearrange("p (n i) d -> p n i d", i=C)
                Q4 = Q_[h][:, :, :].rearrange("p (n i) d -> p n i d", i=C)
                decays = [None] + [SM[h][:, i, :].rearrange("p (n i) -> p n i", i=C) for i in (1, 6, 7)]
                for d in range(h, C):
                    part = NCH if d else NCH // 2
                    w = PD[h][:, d, :].rearrange("p (n i) -> p n i", i=C)[:, :, d:C]
                    for n0 in range(0, NCH, part):
                        T4 = QK[:, 0:part * (C - d) * HD].rearrange("p (n i k) -> p n i k", n=part, i=C - d)
                        link(pool.tensor_tensor(T4, Q4[:, n0:n0 + part, d:C, :], K4[:, n0:n0 + part, 0:C - d, :], ALU.mult))
                        link(pool.tensor_tensor(T4[:, :, :, 0:4], T4[:, :, :, 0:4], T4[:, :, :, 4:8], ALU.add))
                        link(pool.tensor_tensor(T4[:, :, :, 0:2], T4[:, :, :, 0:2], T4[:, :, :, 2:4], ALU.add))
                        link(pool.tensor_tensor(w[:, n0:n0 + part, :].unsqueeze(3), T4[:, :, :, 0:1], T4[:, :, :, 1:2], ALU.add))
                    if d:
                        link(pool.tensor_tensor(w, w, decays[d][:, :, d:C], ALU.mult))
                pool.wait_ge(sem("kk_done", h), 1)
                pool.tensor_tensor(K_[h][:, :, :], K_[h][:, :, :], over(ce), ALU.mult).then_inc(sem("k_decayed", h), 1)
                pool.tensor_tensor(Q_[h][:, :, :], Q_[h][:, :, :], over(cs), ALU.mult).then_inc(sem("q_decayed", h), 1)
            pool.wait_ge(sem("q_decayed", 0), 1)
            pool.wait_ge(sem("q_decayed", 1), 1)

            for g in range(PG):
                for h in range(NHALF):
                    make_products(pool, g, h)
                if g == AT_ROOTS // GC - 1:
                    pool.wait_ge(sem("roots_ready"), 2 * NHALF + 1)
                    scale_outputs(pool, 0)

            def sort_row(s, t):
                pool.indirect_dma_start(sorted_h[s], bass.IndirectOffsetOnAxis(ap=pos[s][:, t:t + 1], axis=0),
                                        H2[s][t // HB][:, t % HB, :], None).then_inc(sem("scattered", s), 16)

            for s in range(NTIME):
                for h in range(NHALF):
                    if s == 0:
                        pool.wait_ge(sem("prod_ready", h), NG // 2 + 1)
                    else:
                        pool.wait_ge(sem("sqo_used"), 2)
                    pool.iota(H2[s][h][:, :, D:D1], [[P, HB], [0, 1]], base=h * HB * P, channel_multiplier=1,
                              allow_small_or_imprecise_dtypes=True).then_inc(sem("place_set"), 1)
                pool.wait_ge(sem("place_set"), NHALF * (s + 1))
                if s == 0:
                    pool.wait_ge(sem("pos_ready", 0), 1)
                    pool.wait_ge(sem("h2_evac"), 4)
                    for t in range(NT):
                        sort_row(0, t)
            for g in range(NTIME * NF):
                pool.wait_ge(sem("ys_ready"), g + 1)
                pool.wait_ge(sem("place_ready"), g + 1)
                pool.indirect_dma_start(placed_y[g // NF], bass.IndirectOffsetOnAxis(ap=place[:, g:g + 1], axis=0),
                                        YS[:, g % YR, :], None).then_inc(sem(f"ys_out{g % YR}"), 16)
                if g == SCAT:
                    pool.wait_ge(sem("pos_ready", 1), 1)
                    pool.wait_ge(sem("h2_evac"), 8)
                    for t in range(NT):
                        sort_row(1, t)

        @block.scalar
        def _(act):
            act.wait_ge(sem("c_in"), 16)
            act.activation(CE[:, :], CROW[:, :], ACT.Silu).then_inc(sem("ce_ready"), 1)
            act.wait_ge(sem("ct_ps"), 1)
            act.activation(CT_[:, :], bank[0][:, 0:B], ACT.Copy).then_inc(sem("ct_ready"), 1)
            act.wait_ge(sem("mod_ps"), 1)
            m4 = bank[1][:, 0:4 * B].rearrange("p (j b) -> p j b", j=4)
            act.activation(MOD[:, :, :], m4, ACT.Copy).then_inc(sem("mod_ready"), 1)
            act.wait_ge(sem("mod_ready"), 1)
            for j in (1, 3):
                act.activation(MOD[:, j, :], MOD[:, j, :], ACT.Identity, bias=1.0).then_inc(sem("mod_ready"), 1)

            roots = [0]

            def root(dst, src):
                roots[0] += 1
                act.wait_ge(sem("root_in"), roots[0])
                act.activation(dst, src, ACT.Sqrt).then_inc(sem("root_out"), 1)

            def modulate(dst, src, k, h, pc, j, done):
                for b2 in range(2):
                    b = h * HB + 2 * pc + b2
                    act.activation(dst[:, k % 2, b2 * N:(b2 + 1) * N], src[:, b2 * N:(b2 + 1) * N], ACT.Identity,
                                   scale=MOD[:, j + 1, b:b + 1], bias=MOD[:, j, b:b + 1]).then_inc(done, 1)

            def shift(k):
                h, pc = divmod(k, PC)
                if k == 0:
                    act.wait_ge(sem("mod_ready"), 3)
                act.wait_ge(sem("xnt_ps"), k + 1)
                if k >= 2:
                    act.wait_ge(sem("proj_ps"), 4 * (k - 1))
                modulate(HT, bank[(0, 7)[k % 2]], k, h, pc, 0, sem("ht_evac"))

            def evacuate(k):
                h = k // PC
                if k + 1 < NHALF * PC:
                    shift(k + 1)
                if k >= 2:
                    act.wait_ge(sem(f"raw_in{k % 2}_", (k - 2) // PC), 64 * ((k - 2) % PC // 2 + 1))
                for i in range(3):
                    act.wait_ge(sem("proj_ps"), 4 * k + i + 1)
                    act.activation(QKV[:, k % 2, :, i, :], bank[1 + i][:, :].rearrange("p (b t) -> p b t", b=2), ACT.Silu if i < 2 else ACT.Copy)\
                        .then_inc(sem("proj_evac", h), 1)
                act.wait_ge(sem("proj_ps"), 4 * k + 4)
                act.activation(BFT[0:2 * H, k % 2, :, :], bank[4][0:2 * H, :].rearrange("p (b t) -> p b t", b=2), ACT.Copy)\
                    .then_inc(sem("proj_evac", h), 1)

            def prepare(h):
                for r in range(2):
                    act.wait_ge(sem(f"raw_in{r}_", h), 64 * PC // 2)
                act.activation(K_[h][:, :, :], RAW[:, :, 1, :].rearrange("p d t -> p t d"), ACT.Square).then_inc(sem("ksq"), 1)
                act.activation(Q_[h][:, :, :], RAW[:, :, 0, :].rearrange("p d t -> p t d"), ACT.Copy).then_inc(sem("q_raw", h), 1)
                act.activation(SM[h][:, 0:2, :], BA[:, :, :], ACT.Sigmoid).then_inc(sem("ba_ready"), 1)
                act.wait_ge(sem("ba_ready"), h + 1)
                act.activation(SM[h][:, 0, :], SM[h][:, 0, :], ACT.Copy, scale=2.0).then_inc(sem("beta_ready", h), 1)
                root(SM[h][:, 3, :], SM[h][:, 2, :])

            root(sd[:, :], ve[:, :])
            shift(0)
            for k in range(NHALF * PC):
                evacuate(k)
                if k == 0:
                    root(sd[:, :], ve[:, :])
                if k == PC:
                    prepare(0)
            prepare(1)

            def ubar(h, n):
                if n >= UR:
                    act.wait_ge(sem("u_ready", h), n - UR + 2)
                act.activation(p1[h][:, n % UR:n % UR + 2, :, :, HD],
                               X_[h][:, n * C:(n + 2) * C, 0:HD].rearrange("p (n i) v -> p n i v", n=2), ACT.Copy)\
                    .then_inc(sem("ubar_in", h), 1)

            def decay(h, n):
                act.wait_ge(sem("s_ready", h), n + 1)
                act.activation(p2[h][:, :, :, C], S_[h][:, n % SR, :, :], ACT.Copy, scale=GAM[h][:, n:n + 1])\
                    .then_inc(sem("decayed", h), 1)

            def out_group(g, h):
                k = g * NHALF + h
                act.wait_ge(sem("o_ps"), k + 1)
                act.wait_ge(sem("s_ready", h), min((g + 1) * GC + 1, NCH))
                act.activation(K_[h][:, g * GC * C:(g + 1) * GC * C, :],
                               bank[6 + k % 2][:, 0:GC * C * HD].rearrange("p (t v) -> p t v", v=HD), ACT.Copy)\
                    .then_inc(sem("o_evac"), 1)

            def squares(s):
                act.wait_ge(sem("o_evac"), (s + 1) * NG // 2 * NHALF)
                if s == 1:
                    for h in range(NHALF):
                        act.wait_ge(sem("prod_ready", h), NG)
                for h in range(NHALF):
                    act.activation(SQO[s][h], K_[h][:, s * P:(s + 1) * P, :], ACT.Square).then_inc(sem("sqo"), 1)

            for h in range(NHALF):
                act.wait_ge(sem("prep_done", h), 1)
                ubar(h, 0)
                ubar(h, 2)
            def rows(k):
                s, q = divmod(k, 4)
                act.wait_ge(sem("h2_ps"), k + 1)
                if k == 4:
                    act.wait_ge(sem("sqo_used"), 2)
                act.activation(H2[s][q // 2][:, q % 2 * 4:q % 2 * 4 + 4, 0:D], BACK_BANKS[s][q][:, :].rearrange("p (n d) -> p n d", n=4), ACT.Copy)\
                    .then_inc(sem("h2_evac"), 1)

            LAGG = 2
            for n in range(NCH):
                if n % 2 == 0 and n >= 2 and n + 2 < NCH:
                    for h in range(NHALF):
                        ubar(h, n + 2)
                for h in range(NHALF):
                    if n < NCH - 1:
                        decay(h, n)
                if n % GC == GC - 1 and n // GC >= LAGG:
                    for h in range(NHALF):
                        out_group(n // GC - LAGG, h)
                if n == AT_SQUARES:
                    squares(0)
                if n == AT_SUMS + 1:
                    root(sm[:, 3, :], sm[:, 2, :])
                if n == AT_STATS + 3:
                    root(sd[:, :], ve[:, :])
                if AT_ROWS + 2 <= n < AT_ROWS + 6:
                    rows(n - AT_ROWS - 2)
            def exponentials(s):
                act.wait_ge(sem("lsub"), s + 1)
                act.activation(ex[:, :, :], ex[:, :, :], ACT.Exp).then_inc(sem("lexp"), 1)

            def gate_evac(q):
                act.wait_ge(sem("gb_ps"), q + 1)
                act.activation(GB[:, 4 * q:4 * q + 4, :], bank[5][:, :].rearrange("p (n d) -> p n d", n=4), ACT.Copy)\
                    .then_inc(sem("gb_evac"), 1)

            for g in range(NG - LAGG, NG):
                for h in range(NHALF):
                    out_group(g, h)
            squares(1)
            root(sm[:, 3, :], sm[:, 2, :])
            exponentials(0)

            G = NTIME * NF

            def silu(g):
                act.wait_ge(sem("h_ps"), 2 * g + 1)
                if g >= 2:
                    act.wait_ge(sem("gut_ps"), g - 1)
                act.activation(GU[:, g % 2, :], bank[(1, 6)[g % 2]][:, :], ACT.Silu).then_inc(sem("silu_a"), 1)

            def gut(g):
                act.wait_ge(sem("gut_ps"), g + 1)
                if g >= 2:
                    act.wait_ge(sem("y_ps"), g - 1)
                act.activation(GUT[:, g % 2, :], bank[3][:, :], ACT.Copy).then_inc(sem("gut_ready"), 1)

            for g in range(G + 1):
                if g < G:
                    silu(g)
                if g >= 1:
                    gut(g - 1)
                if F_GATES < g <= F_GATES + 4:
                    gate_evac(g - F_GATES - 1)
                if g == F_ROOT:
                    root(sd[:, :], ve[:, :])
                if F_TURN < g <= F_TURN + 4:
                    rows(g - F_TURN + 3)
                if g == F_TURN + 5:
                    exponentials(1)

        @block.vector
        def _(dve):
            done = [0]

            def link(ins):
                done[0] += 1
                ins.then_inc(sem("dve_link"), 1)
                dve.wait_ge(sem("dve_link"), done[0])

            roots = [0]

            def ask_root(var, t):
                roots[0] += 1
                dve.tensor_copy(t, var).then_inc(sem("root_in"), 1)
                dve.wait_ge(sem("root_in"), roots[0])

            def rsqrt(var, sroot, y, t):
                dve.wait_ge(sem("root_out"), roots[0])
                link(dve.reciprocal(y, sroot))
                link(dve.tensor_tensor(t, y, y, ALU.mult))
                link(dve.tensor_tensor(t, t, var, ALU.mult))
                link(dve.tensor_scalar(t, t, -0.5, 1.5, ALU.mult, ALU.add))
                dve.tensor_tensor(y, y, t, ALU.mult).then_inc(sem("roots_ready"), 1)
                dve.wait_ge(sem("roots_ready"), roots[0])

            def stats(tile, ready, tiles):
                for t in tiles:
                    T = tile(t)
                    if ready == "xn_ready" and T % 4 == 0:
                        dve.wait_ge(sem(f"x_in{T // 4}"), 16)
                    last = dve.bn_stats(st[:, t, :], X[:, T, :])
                link(last)

            def variances():
                for t in range(NT):
                    last = dve.bn_aggr(mv[:, t, :], st[:, t, :])
                link(last)
                link(dve.tensor_scalar(ve[:, :], mv[:, :, 1], LN_EPS, None, ALU.add))
                ask_root(ve[:, :], y2[:, :])

            def scale(h, tile, XN, ready, tiles):
                if ready == "xn2_ready" and h == 1:
                    dve.wait_ge(sem("xn2t_ps"), 4)
                for t in tiles:
                    dve.tensor_scalar(XN[:, t, :], X[:, tile(t), :], mv[:, t, 0:1], yy[:, t:t + 1], ALU.subtract, ALU.mult)\
                        .then_inc(sem(ready, h), 1)

            def normalise(h):
                def tile(t):
                    return h * NT + t
                stats(tile, "xn_ready", range(NT))
                variances()
                rsqrt(ve[:, :], sd[:, :], yy[:, :], y2[:, :])
                scale(h, tile, XN[h], "xn_ready", range(NT))

            normalise(0)
            dve.wait_ge(sem("w_in"), 16 * 5)
            dve.tensor_copy(WBF[:, :, :], WBFR[:, :, :].rearrange("p x h -> p h x")).then_inc(sem("wbf_ready"), 1)
            dve.wait_ge(sem("gate_ps"), 1)
            g2 = bank[5][0:B, 0:2 * D].rearrange("p (j d) -> p j d", j=2)
            link(dve.tensor_copy(GATE[:, :, :], g2))
            link(dve.tensor_scalar(GTMP[:, :, :], GATE[:, :, :], -1.0, 0.25, ALU.mult, ALU.max))
            link(dve.tensor_tensor(GTMP[:, :, :], GTMP[:, :, :], GATE[:, :, :], ALU.max))
            link(dve.tensor_scalar(GATE[:, :, :], GATE[:, :, :], 0.0, 2.0, ALU.is_ge, ALU.mult))
            link(dve.tensor_scalar(GATE[:, :, :], GATE[:, :, :], -1.0, None, ALU.add))
            dve.tensor_tensor(GATE[:, :, :], GATE[:, :, :], GTMP[:, :, :], ALU.mult).then_inc(sem("gate_ready"), 1)
            normalise(1)

            def prepare(h):
                K, XX = K_[h], X_[h]
                beta, a, n2, rt, rn, t_, d2, d3 = (SM[h][:, i, :] for i in range(8))
                K4 = K[:, :, :].rearrange("p (n i) d -> p n i d", i=C)
                X4 = XX[:, :, :].rearrange("p (n i) d -> p n i d", i=C)

                def at(v, i, j=None):
                    return v.rearrange("p (n i) -> p n i", i=C)[:, :, i:(j or i + 1)]

                dve.wait_ge(sem("ksq"), h + 1)
                link(dve.tensor_reduce(n2, K[:, :, :], AX_X, ALU.add))
                link(dve.tensor_scalar(n2, n2, K_EPS, None, ALU.add))
                ask_root(n2, t_)
                rsqrt(n2, rt, rn, t_)
                dve.tensor_tensor(K[:, :, :], RAW[:, :, 1, :].rearrange("p d t -> p t d"), over(rn), ALU.mult)\
                    .then_inc(sem("raw_used"), 1)
                dve.wait_ge(sem("beta_ready", h), 1)
                dve.wait_ge(sem("raw_used"), h + 1)
                link(dve.tensor_tensor(at(d2, 1, C), at(a, 1, C), at(a, 0, C - 1), ALU.mult))
                link(dve.tensor_tensor(at(d3, 2, C), at(d2, 2, C), at(a, 0, C - 2), ALU.mult))
                decays = [None, a, d2, d3]
                cs, ce = n2, rt
                link(dve.tensor_copy(at(cs, 0), at(a, 0)))
                for i in range(1, C):
                    link(dve.tensor_tensor(at(cs, i), at(cs, i - 1), at(a, i), ALU.mult))
                link(dve.memset(at(ce, C - 1), 1.0))
                for i in range(C - 2, -1, -1):
                    link(dve.tensor_tensor(at(ce, i), at(ce, i + 1), at(a, i + 1), ALU.mult))
                link(dve.scalar_tensor_tensor(out=rn, in0=beta, scalar=-1.0, in1=cs, op0=ALU.mult, op1=ALU.mult))
                dve.tensor_copy(GAM[h][:, :].unsqueeze(2), at(cs, C - 1)).then_inc(sem("decays_ready", h), 1)
                dve.wait_ge(sem("decays_ready", h), 1)
                Lf = L[:, :, :]
                for d in range(1, C):
                    T4 = TMP[:, 0:NCH * (C - d) * HD].rearrange("p (n i k) -> p n i k", n=NCH, i=C - d)
                    last_kk = dve.tensor_tensor(T4, K4[:, :, d:C, :], K4[:, :, 0:C - d, :], ALU.mult)
                    if h == 0 and d == C - 1:
                        last_kk.then_inc(sem("kk_done", h), 1)
                        dve.wait_ge(sem("kk_done", h), 1)
                    else:
                        link(last_kk)
                    diag = Lf[:, :, C * d:C * C:C + 1]
                    link(dve.tensor_reduce(diag, T4, AX_X, ALU.add))
                    w = at(t_, d, C)
                    link(dve.tensor_tensor(w, at(decays[d], d, C), at(beta, d, C), ALU.mult))
                    link(dve.tensor_tensor(diag, diag, w, ALU.mult))
                if h == 1:
                    dve.wait_ge(sem("q_raw", h), 1)
                    T3 = TMP[:, 0:N * HD].rearrange("p (t k) -> p t k", k=HD)
                    dve.tensor_tensor(T3, Q_[h][:, :, :], K[:, :, :], ALU.mult).then_inc(sem("kk_done", h), 1)
                    dve.wait_ge(sem("kk_done", h), 1)
                    link(dve.tensor_reduce(PD[h][:, 0, :], T3, AX_X, ALU.add))
                dve.wait_ge(sem("uw_started", h), 2)
                for j in range(C - 1):
                    m = C - 1 - j
                    T4 = TMP[:, 0:NCH * m * 2 * HD].rearrange("p (n i x) -> p n i x", n=NCH, i=m)
                    col = Lf[:, :, C * (j + 1) + j:C * C:C]
                    link(dve.tensor_tensor(T4, col.unsqueeze(3).broadcast_to([P, NCH, m, 2 * HD]),
                                           X4[:, :, j:j + 1, :].broadcast_to([P, NCH, m, 2 * HD]), ALU.mult))
                    ins = dve.tensor_tensor(X4[:, :, j + 1:C, :], X4[:, :, j + 1:C, :], T4, ALU.subtract)
                    if j < C - 2:
                        link(ins)
                    else:
                        ins.then_inc(sem("prep_done", h), 1)
                        dve.wait_ge(sem("prep_done", h), 1)

            for s in range(NTIME):
                dve.wait_ge(sem("padded", s), 16)
            prepare(0)
            for r in range(2):
                dve.wait_ge(sem(f"raw_in{r}_", 1), 64 * PC // 2)
            for b in range(B):
                if b == 0:
                    dve.wait_ge(sem("wo_in"), 16 * 4)
                if b % 4 == 0:
                    dve.wait_ge(sem("ga_ps"), b // 4 + 1)
                dve.scalar_tensor_tensor(out=WOG[:, b, :], in0=bank[(5, 6, 0, 7)[b // 4]][:, b % 4 * D:(b % 4 + 1) * D], scalar=NW[:, 0:1],
                                         in1=WO[:, :], op0=ALU.mult, op1=ALU.mult).then_inc(sem("wog_ready"), 1)
            prepare(1)

            for h in range(NHALF):
                dve.memset(S_[h][:, 0, :, :], 0.0).then_inc(sem("s_ready", h), 1)

            def from_state(h, n):
                dve.wait_ge(sem("s_ready", h), n + 1)
                s_ = S_[h][:, n % SR, :, :].unsqueeze(1).broadcast_to([P, C, HD, HD])
                w = X_[h][:, n * C:(n + 1) * C, HD:2 * HD].unsqueeze(2).broadcast_to([P, C, HD, HD])
                dve.tensor_tensor(p1[h][:, n % UR, :, :, 0:HD], s_, w, ALU.mult).then_inc(sem("seq_w", h), 1)

            def sum_u(h, n):
                dve.wait_ge(sem("seq_w", h), n + 1)
                dve.wait_ge(sem("ubar_in", h), n // 2 + 1)
                dve.tensor_reduce(X_[h][:, n * C:(n + 1) * C, 0:HD], p1[h][:, n % UR, :, :, :], AX_X, ALU.add)\
                    .then_inc(sem("u_ready", h), 1)

            def outer(h, n):
                if n == 0:
                    dve.wait_ge(sem("k_decayed", h), 1)
                dve.wait_ge(sem("u_ready", h), n + 1)
                u = X_[h][:, n * C:(n + 1) * C, 0:HD].rearrange("p i v -> p v i").unsqueeze(2).broadcast_to([P, HD, HD, C])
                k = K_[h][:, n * C:(n + 1) * C, :].rearrange("p i k -> p k i").unsqueeze(1).broadcast_to([P, HD, HD, C])
                dve.tensor_tensor(p2[h][:, :, :, 0:C], u, k, ALU.mult).then_inc(sem("seq_k", h), 1)

            def next_state(h, n):
                dve.wait_ge(sem("seq_k", h), n + 1)
                dve.wait_ge(sem("decayed", h), n + 1)
                if n + 1 >= SR:
                    dve.wait_ge(sem("prod_ready", h), (n + 1 - SR) // GC + 1)
                dve.tensor_reduce(S_[h][:, (n + 1) % SR, :, :], p2[h][:, :, :, :], AX_X, ALU.add).then_inc(sem("s_ready", h), 1)

            def sums_of_squares(s):
                ms = sm[:, 2, :]
                for h in range(NHALF):
                    dve.wait_ge(sem("sqo"), 2 * s + h + 1)
                    last = dve.tensor_reduce(ms[:, h * P:(h + 1) * P], SQO[s][h], AX_X, ALU.add)
                last.then_inc(sem("sqo_used"), 1)
                dve.wait_ge(sem("sqo_used"), s + 1)
                link(dve.tensor_scalar(ms, ms, 1.0 / HD, O_EPS, ALU.mult, ALU.add))
                ask_root(ms, sm[:, 5, :])

            def attend(s, q):
                dve.wait_ge(sem("att_ps", s), q + 1)
                xr = XG[s][:, 4 * q:4 * q + 4, :]
                dve.tensor_tensor(xr, xr, ATT_BANKS[s][q][:, :].rearrange("p (n d) -> p n d", n=4), ALU.add)\
                    .then_inc(sem("x1_ready", s), 1)

            def logits():
                dve.wait_ge(sem("lg_ps", 0), 4)
                dve.tensor_tensor(lg[:, :, :], bank[5][:, 0:NT * E].rearrange("p (t e) -> p t e", e=E),
                                  RB[:, :].unsqueeze(1).broadcast_to([P, NT, E]), ALU.add).then_inc(sem("lg_ready", 0), 1)
                dve.wait_ge(sem("lg_ready", 0), 1)

            def logits_part(q):
                dve.wait_ge(sem("lg_ps", 1), q + 1)
                dve.tensor_tensor(lg[:, 4 * q:4 * q + 4, :], bank[4][:, 0:4 * E].rearrange("p (t e) -> p t e", e=E),
                                  RB[:, :].unsqueeze(1).broadcast_to([P, 4, E]), ALU.add).then_inc(sem("lg_part"), 1)

            def route(s):
                l3 = [P, NT, E]
                if s == 1:
                    dve.wait_ge(sem("lg_part"), 4)
                link(dve.tensor_reduce(lmx[:, :], lg[:, :, :], AX_X, ALU.max))
                top = lmx[:, :].unsqueeze(2).broadcast_to(l3)
                dve.tensor_tensor(ex[:, :, :], lg[:, :, :], top, ALU.subtract).then_inc(sem("lsub"), 1)
                link(dve.tensor_tensor(oh[:, :, :], lg[:, :, :], top, ALU.is_equal))
                link(dve.tensor_tensor(oh[:, :, :], oh[:, :, :], rev[:, :].unsqueeze(1).broadcast_to(l3), ALU.mult))
                link(dve.tensor_reduce(lm[:, :], oh[:, :, :], AX_X, ALU.max))
                dve.tensor_tensor(oh[:, :, :], rev[:, :].unsqueeze(1).broadcast_to(l3), lm[:, :].unsqueeze(2).broadcast_to(l3), ALU.is_equal)\
                    .then_inc(sem("oh_ready", s), 1)

            def probability(s):
                dve.wait_ge(sem("lexp"), s + 1)
                link(dve.tensor_reduce(posf[:, :], ex[:, :, :], AX_X, ALU.add))
                link(dve.reciprocal(maxp[s][:, :], posf[:, :]))

            def sort(s):
                ranks = bank[4]
                dve.wait_ge(sem("rank_ps", s), 1)
                link(dve.tensor_copy(tot[:, :, :], ranks[:, NT * E:2 * NT * E].rearrange("p (t e) -> p e t", e=E)))
                flat = "p e t -> p (e t)"
                link(dve.tensor_tensor_scan(exc[:, :, :].rearrange(flat), msk[:, :, :].rearrange(flat),
                                            tot[:, :, :].rearrange(flat), 0.0, ALU.mult, ALU.add))
                cnt = exc[:, :, NT - 1:NT]
                link(dve.tensor_tensor(cmn[:, :, :], cnt.broadcast_to([P, E, NT]), i128[:, :].unsqueeze(1).broadcast_to([P, E, NT]), ALU.is_gt))
                link(dve.tensor_reduce(nt8[:, :], cmn[:, :, :], AX_X, ALU.add))
                link(dve.tensor_tensor_scan(cu8[:, :], one8[:, :], nt8[:, :], 0.0, ALU.mult, ALU.add))
                link(dve.tensor_tensor(ba8[:, :], cu8[:, :], nt8[:, :], ALU.subtract))
                link(dve.tensor_scalar(ba8[:, :], ba8[:, :], float(P), None, ALU.mult))
            def tiles_experts(s):
                link(dve.tensor_tensor(cmp[:, :, :], ij[:, :].unsqueeze(2).broadcast_to([P, NF, E]),
                                       cu8[:, :].unsqueeze(1).broadcast_to([P, NF, E]), ALU.is_ge))
                link(dve.tensor_reduce(texf[:, :], cmp[:, :, :], AX_X, ALU.add))
                dve.tensor_scalar(tex[s][:, :], texf[:, :], float(E - 1), None, ALU.min).then_inc(sem("tex_ready", s), 1)
            def sorted_places(s):
                ranks = bank[4]
                link(dve.tensor_tensor(exc[:, :, :], exc[:, :, :], tot[:, :, :], ALU.subtract))
                link(dve.tensor_tensor(exc[:, :, :], exc[:, :, :], ba8[:, :].unsqueeze(2).broadcast_to([P, E, NT]), ALU.add))
                link(dve.tensor_tensor(t8[:, :, :], exc[:, :, :].rearrange("p e t -> p t e"),
                                       ranks[:, 0:NT * E].rearrange("p (t e) -> p t e", e=E), ALU.add))
                link(dve.tensor_tensor(t8[:, :, :], t8[:, :, :], oh[:, :, :], ALU.mult))
                link(dve.tensor_reduce(posf[:, :], t8[:, :, :], AX_X, ALU.add))
                dve.tensor_copy(pos[s][:, :], posf[:, :]).then_inc(sem("pos_ready", s), 1)
                dve.wait_ge(sem("pos_ready", s), 1)

            def shift2(k):
                dve.wait_ge(sem("xn2t_ps"), k + 1)
                if k >= 2:
                    dve.wait_ge(sem("h2_ps"), k - 1)
                for i in range(4):
                    b = 4 * (k % 4) + i
                    dve.tensor_scalar(H2T[:, k % 2, i * P:(i + 1) * P], TURN_BANKS[k // 4][k % 4][:, i * P:(i + 1) * P],
                                      MOD[:, 3, b:b + 1], MOD[:, 2, b:b + 1], ALU.mult, ALU.add).then_inc(sem("shifted"), 1)

            def first_tile(t):
                return NTIME * t

            def second_tile(t):
                return NTIME * t + 1

            for n in range(NCH):
                for step in (from_state, sum_u, outer, next_state):
                    if step in (outer, next_state) and n == NCH - 1:
                        continue
                    for h in range(NHALF):
                        step(h, n)
                if n == AT_SUMS:
                    sums_of_squares(0)
                if n == AT_ROOTS:
                    rsqrt(*(sm[:, i, :] for i in (2, 3, 4, 5)))
                if n == AT_ATTEND:
                    for q in range(4):
                        attend(0, q)
                    dve.wait_ge(sem("x1_ready", 0), 4)
                if n in (AT_STATS, AT_STATS + 1):
                    half = (n - AT_STATS) * NT // 2
                    stats(first_tile, "xn2_ready", range(half, half + NT // 2))
                if n == AT_STATS + 2:
                    variances()
                if n == AT_ROWS:
                    rsqrt(ve[:, :], sd[:, :], yy[:, :], y2[:, :])
                    scale(0, first_tile, XNB, "xn2_ready", range(NT))
                if AT_ROWS < n <= AT_ROWS + 4:
                    shift2(n - AT_ROWS - 1)
                if n == AT_ROWS + 5:
                    logits()
                    route(0)
                if n == AT_ROWS + 7:
                    sort(0)
                    sorted_places(0)
                    tiles_experts(0)

            for g in range(PG, NG):
                for h in range(NHALF):
                    make_products(dve, g, h)
            sums_of_squares(1)
            rsqrt(*(sm[:, i, :] for i in (2, 3, 4, 5)))
            scale_outputs(dve, 1)

            G = NTIME * NF

            def xst(g):
                dve.wait_ge(sem("xt_ps"), g + 1)
                if g >= 2:
                    dve.wait_ge(sem("h_ps"), 2 * (g - 1))
                dve.tensor_copy(XST[:, g % 2, :], bank[0][:, 0:P]).then_inc(sem("xst_ready"), 1)
                dve.wait_ge(sem(f"xs_in{g % XR}"), 16 * (g // XR + 1))
                dve.tensor_copy(place[:, g:g + 1], XS[:, g % XR, D:D1]).then_inc(sem("place_ready"), 1)

            def gate_u(g):
                dve.wait_ge(sem("silu_a"), g + 1)
                dve.wait_ge(sem("h_ps"), 2 * g + 2)
                dve.tensor_tensor(GU[:, g % 2, :], GU[:, g % 2, :], bank[(2, 7)[g % 2]][:, :], ALU.mult)\
                    .then_inc(sem("gu_ready"), 1)

            def ys(g):
                dve.wait_ge(sem("y_ps"), g + 1)
                if g >= YR:
                    dve.wait_ge(sem(f"ys_out{g % YR}"), 16 * (g // YR))
                dve.tensor_copy(YS[:, g % YR, :], bank[0][:, P:P + D]).then_inc(sem("ys_ready"), 1)

            def finish(s, q):
                dve.wait_ge(sem(f"y_in{q}"), 16 * (s + 1))
                yg = YG[s][q // 2]
                if s == 0:
                    for b in range(4 * q, 4 * q + 4):
                        last = dve.scalar_tensor_tensor(out=yg[:, b % HB, :], in0=yg[:, b % HB, :], scalar=maxp[s][:, b:b + 1],
                                                        in1=GB[:, b, :], op0=ALU.mult, op1=ALU.mult)
                else:
                    y4 = yg[:, q % 2 * 4:q % 2 * 4 + 4, :]
                    last = dve.tensor_tensor(y4, y4, GB[:, 4 * q:4 * q + 4, :], ALU.mult)
                last.then_inc(sem("y_scaled"), 1)
                dve.wait_ge(sem("y_scaled"), 4 * s + q + 1)
                xr = XG[s][:, 4 * q:4 * q + 4, :]
                dve.tensor_tensor(xr, xr, yg[:, q % 2 * 4:q % 2 * 4 + 4, :], ALU.add).then_inc(sem("out_ready", s), 1)

            xst(0)
            for g in range(G + 2):
                if g + 1 < G:
                    xst(g + 1)
                if F_TURN <= g < F_TURN + 4:
                    shift2(g - F_TURN + 4)
                if g < G:
                    gate_u(g)
                if g >= 2:
                    ys(g - 2)
                if g == 0:
                    probability(0)
                if g in (F_ATTEND + 1, F_ATTEND + 2):
                    for q in (2 * (g - F_ATTEND - 1), 2 * (g - F_ATTEND - 1) + 1):
                        attend(1, q)
                    dve.wait_ge(sem("x1_ready", 1), 2 * (g - F_ATTEND))
                if g in (F_ATTEND + 1, F_ATTEND + 3):
                    half = (g - F_ATTEND - 1) * NT // 4
                    stats(second_tile, "xn2_ready", range(half, half + NT // 2))
                if g == F_ATTEND + 4:
                    variances()
                if g == F_ROOT:
                    rsqrt(ve[:, :], sd[:, :], yy[:, :], y2[:, :])
                    scale(1, second_tile, XNB, "xn2_ready", range(NT // 2))
                if g == F_ROOT + 1:
                    scale(1, second_tile, XNB, "xn2_ready", range(NT // 2, NT))
                if F_TURN <= g < F_TURN + 4:
                    logits_part(g - F_TURN)
                if g == F_TURN + 4:
                    route(1)
                if g == F_TURN + 5:
                    sort(1)
                if g == F_TURN + 6:
                    sorted_places(1)
                if g == F_TURN + 7:
                    tiles_experts(1)
                    probability(1)
                if NF + YIN - 2 <= g < NF + YIN + 2:
                    finish(0, g - NF - YIN + 2)
                if NF + YIN + 2 <= g < NF + YIN + 6:
                    for b in range(4 * (g - NF - YIN - 2), 4 * (g - NF - YIN - 1)):
                        link(dve.tensor_scalar(GB[:, b, :], GB[:, b, :], maxp[1][:, b:b + 1], None, ALU.mult))
            for q in range(4):
                finish(1, q)


_INS = ["L0_attn_x", "L0_attn_Wq", "L0_attn_Wk", "L0_attn_Wv", "L0_attn_Wo", "L0_attn_Wbet", "L0_attn_Wf", "L0_attn_norm_w",
        "L0_ffn_router_w", "L0_ffn_router_b", "L0_ffn_w1", "L0_ffn_w2", "L0_c", "L0_wmod"]
_OUTS = [((16, 256, 128), "float32")]


def kernel(**inputs):
    import numpy as _np
    import concourse.bacc as _bacc
    from concourse import mybir as _mybir
    from concourse.bass_utils import run_bass_kernel_spmd as _run

    nc = _bacc.Bacc("TRN2", target_bir_lowering=False, num_devices=1)
    arrays, args = {}, []
    for name in _INS:
        a = _np.ascontiguousarray(inputs[name])
        arrays[f"in_{name}_dram"] = a
        args.append(nc.dram_tensor(f"in_{name}_dram", a.shape, _mybir.dt.from_np(a.dtype), kind="ExternalInput").ap())
    for i, (shape, dtype) in enumerate(_OUTS):
        dt = _mybir.dt.from_np(_np.dtype(dtype))
        args.append(nc.dram_tensor(f"out_{i}_dram", shape, dt, kind="ExternalOutput").ap())
    adaln_block(nc, *args)
    r = _run(nc, [arrays], core_ids=[0])
    got = tuple(r.results[0][f"out_{i}_dram"] for i in range(len(_OUTS)))
    return got[0]
```
